# Optimizing a Trainium2 kernel written in Bass

```python
import numpy as np
import jax
import jax.numpy as jnp

def _softmax(x, axis=-1):
    return jax.nn.softmax(x, axis=axis)

def _gelu(x):
    return jax.nn.gelu(x, approximate=True)

def _silu(x):
    return jax.nn.silu(x)

def _sigmoid(x):
    return jax.nn.sigmoid(x)

def _layernorm(x, axis=-1, eps=1e-05):
    m = jnp.mean(x, axis=axis, keepdims=True)
    v = jnp.var(x, axis=axis, keepdims=True)
    return (x - m) / jnp.sqrt(v + eps)

def _scatter_add(tgt, idx, src, axis=0):
    return tgt.at[idx].add(src)

def _segment_sum(src, seg, n):
    return jax.ops.segment_sum(src, seg, n)
kernel_name = 'mk_sandwich_d1_jaxref_r4_1c79d3'

def setup_inputs(seed: int=0):
    np.random.seed(seed)
    _w = jnp.asarray

    def _L0_attn_setup():
        import jax, jax.numpy as jnp
        import numpy as np
        DIM = 256
        HEADS = 1
        HDIM = DIM // HEADS
        INNER = 16
        B, L = (2, 1024)
        ROPE_BASE = 32.0

        def _apply_rope(x, pos, base):
            d = x.shape[-1]
            inv_freq = base ** (-jnp.arange(0, d, 2, dtype=jnp.float32) / d)
            ang = pos[:, None].astype(jnp.float32) * inv_freq
            emb = jnp.concatenate([ang, ang], axis=-1)
            cos = jnp.cos(emb)[None, :, None, :].astype(x.dtype)
            sin = jnp.sin(emb)[None, :, None, :].astype(x.dtype)
            x1, x2 = (x[..., :d // 2], x[..., d // 2:])
            rot = jnp.concatenate([-x2, x1], axis=-1)
            return x * cos + rot * sin
        key = jax.random.key(seed)
        ks = jax.random.split(key, 7)
        hidden_states = jax.random.normal(ks[0], (B, L, DIM), dtype=jnp.float32)
        Wq = jax.random.normal(ks[1], (DIM, DIM), dtype=jnp.float32) * 0.02
        Wk = jax.random.normal(ks[2], (DIM, DIM), dtype=jnp.float32) * 0.02
        fc1_w = jax.random.normal(ks[3], (INNER, 1), dtype=jnp.float32) * 0.1
        fc1_b = jax.random.normal(ks[4], (INNER,), dtype=jnp.float32) * 0.1
        fc2_w = jax.random.normal(ks[5], (DIM, INNER), dtype=jnp.float32) * 0.1
        fc2_b = jax.random.normal(ks[6], (DIM,), dtype=jnp.float32) * 0.1
        return {'hidden_states': hidden_states, 'Wq': Wq, 'Wk': Wk, 'fc1_w': fc1_w, 'fc1_b': fc1_b, 'fc2_w': fc2_w, 'fc2_b': fc2_b}
    _L0_attn_in = _L0_attn_setup()

    def _L0_ffn_setup():
        import jax, jax.numpy as jnp
        import numpy as np
        from jax import lax
        D = 256
        E = 8
        F = 1024
        TOP_K = 2
        key = jax.random.key(seed)
        ks = jax.random.split(key, 8)
        s = 0.02
        return {'x': jax.random.normal(ks[0], (4, 512, D), dtype=jnp.float32), 'gate_w': jax.random.normal(ks[1], (D, E), dtype=jnp.float32) * s, 'gate_b': jnp.zeros((E,), dtype=jnp.float32), 'w1': jax.random.normal(ks[2], (E, D, F), dtype=jnp.float32) * s, 'b1': jnp.zeros((E, F), dtype=jnp.float32), 'w2': jax.random.normal(ks[3], (E, F, D), dtype=jnp.float32) * s, 'b2': jnp.zeros((E, D), dtype=jnp.float32)}
    _L0_ffn_in = _L0_ffn_setup()
    _d = {'L0_attn_hidden_states': _L0_attn_in['hidden_states'], 'L0_attn_Wq': _L0_attn_in['Wq'], 'L0_attn_Wk': _L0_attn_in['Wk'], 'L0_attn_fc1_w': _L0_attn_in['fc1_w'], 'L0_attn_fc1_b': _L0_attn_in['fc1_b'], 'L0_attn_fc2_w': _L0_attn_in['fc2_w'], 'L0_attn_fc2_b': _L0_attn_in['fc2_b'], 'L0_ffn_gate_w': _L0_ffn_in['gate_w'], 'L0_ffn_gate_b': _L0_ffn_in['gate_b'], 'L0_ffn_w1': _L0_ffn_in['w1'], 'L0_ffn_b1': _L0_ffn_in['b1'], 'L0_ffn_w2': _L0_ffn_in['w2'], 'L0_ffn_b2': _L0_ffn_in['b2']}
    _x0 = _d['L0_attn_hidden_states']
    _d['L0_attn_hidden_states'] = jax.random.normal(jax.random.fold_in(jax.random.key(seed), 1), (4, 1024, 256), dtype=_x0.dtype)
    del _x0
    return _d

def reference(L0_attn_hidden_states, L0_attn_Wq, L0_attn_Wk, L0_attn_fc1_w, L0_attn_fc1_b, L0_attn_fc2_w, L0_attn_fc2_b, L0_ffn_gate_w, L0_ffn_gate_b, L0_ffn_w1, L0_ffn_b1, L0_ffn_w2, L0_ffn_b2):

    def _L0_attn_ref(hidden_states, Wq, Wk, fc1_w, fc1_b, fc2_w, fc2_b):
        import jax, jax.numpy as jnp
        import numpy as np
        DIM = 256
        HEADS = 1
        HDIM = DIM // HEADS
        INNER = 16
        B, L = (2, 1024)
        ROPE_BASE = 32.0

        def _apply_rope(x, pos, base):
            d = x.shape[-1]
            inv_freq = base ** (-jnp.arange(0, d, 2, dtype=jnp.float32) / d)
            ang = pos[:, None].astype(jnp.float32) * inv_freq
            emb = jnp.concatenate([ang, ang], axis=-1)
            cos = jnp.cos(emb)[None, :, None, :].astype(x.dtype)
            sin = jnp.sin(emb)[None, :, None, :].astype(x.dtype)
            x1, x2 = (x[..., :d // 2], x[..., d // 2:])
            rot = jnp.concatenate([-x2, x1], axis=-1)
            return x * cos + rot * sin
        b, l, _ = hidden_states.shape
        q = (hidden_states @ Wq.T).reshape(b, l, HEADS, HDIM).astype(jnp.bfloat16)
        k = (hidden_states @ Wk.T).reshape(b, l, HEADS, HDIM).astype(jnp.bfloat16)
        pos = jnp.arange(l)
        q = _apply_rope(q, pos, ROPE_BASE)
        k = _apply_rope(k, pos, ROPE_BASE)
        scores = jnp.einsum('bqhd,bkhd->bhqk', q.astype(jnp.float32), k.astype(jnp.float32)) / HDIM ** 0.5
        causal = jnp.tril(jnp.ones((l, l), dtype=bool))
        exp_qk = jnp.where(causal[None, None], jnp.exp(scores), 0.0)
        o = jnp.swapaxes(exp_qk.sum(axis=-1), 1, 2)
        o = jax.nn.relu(o @ fc1_w.T + fc1_b)
        return o @ fc2_w.T + fc2_b

    def _L0_ffn_ref(x, gate_w, gate_b, w1, b1, w2, b2):
        import jax, jax.numpy as jnp
        import numpy as np
        from jax import lax
        D = 256
        E = 8
        F = 1024
        TOP_K = 2
        B, S, _ = x.shape
        flat = x.reshape(-1, D)
        T = flat.shape[0]
        logits = flat @ gate_w + gate_b
        topv, topi = lax.top_k(logits, TOP_K)
        topw = jax.nn.softmax(topv.astype(jnp.float32), axis=-1).astype(x.dtype)
        routing = jnp.zeros_like(logits).at[jnp.arange(T)[:, None], topi].set(topw)

        def body(acc, params):
            W1e, b1e, W2e, b2e, we = params
            h = jax.nn.gelu(flat @ W1e + b1e, approximate=False)
            out = h @ W2e + b2e
            return (acc + out * we[:, None], None)
        init = jnp.zeros_like(flat)
        final, _ = lax.scan(body, init, (w1, b1, w2, b2, routing.T))
        return final.reshape(B, S, D)
    x = L0_attn_hidden_states
    x = x + _layernorm(_L0_attn_ref(_layernorm(x, axis=-1), L0_attn_Wq, L0_attn_Wk, L0_attn_fc1_w, L0_attn_fc1_b, L0_attn_fc2_w, L0_attn_fc2_b), axis=-1)
    x = x + _layernorm(_L0_ffn_ref(_layernorm(x, axis=-1), L0_ffn_gate_w, L0_ffn_gate_b, L0_ffn_w1, L0_ffn_b1, L0_ffn_w2, L0_ffn_b2), axis=-1)
    return x

_drawn_inputs = setup_inputs


def setup_inputs(seed=0):
    import zlib

    import numpy as np

    out = dict(_drawn_inputs(seed))
    spreads = {'L0_ffn_gate_b': (0.0, 0.1), 'L0_ffn_b1': (0.0, 0.1), 'L0_ffn_b2': (0.0, 0.1)}
    factors = {'L0_attn_Wq': 8.0, 'L0_attn_Wk': 8.0}
    for name, (base, spread) in spreads.items():
        noise = np.random.default_rng([zlib.crc32(name.encode()), seed]).standard_normal(out[name].shape)
        drawn = base * np.exp(spread * noise) if base else spread * noise
        out[name] = jnp.asarray(drawn.astype(out[name].dtype))
    for name, factor in factors.items():
        out[name] = (out[name] * factor).astype(out[name].dtype)
    return out
```

```python
from contextlib import ExitStack

import numpy as np
import concourse.bass as bass
from concourse import mybir

F32 = mybir.dt.float32
F32R = mybir.dt.float32r
BF16 = mybir.dt.bfloat16
I32 = mybir.dt.int32
U32 = mybir.dt.uint32
ALU = mybir.AluOpType
ACT = mybir.ActivationFunctionType
AX_X = mybir.AxisListType.X

P = 128
EPS = 1e-5
RSQRT_MAGIC = float(0x5F3759DF)
MASKED = -1e30

B, L, D = 4, 1024, 256
NT = B * L
KC = D // P
TB = L // P
TT = NT // P
INNER = 16
HID = 32
NE, F = 8, 1024
FC = F // P
TM = 256
TPE = NT // TM
GRP = 4
MAXG = 2 * NT // TM + NE
REGION = NT + TM
XW = D + 4
NO_TOKEN = 4.0 * NT

ONE = 1

C_END, C_TILES, C_BASE, C_ROW = 0, NE, 2 * NE, 3 * NE
TAB = MAXG + TPE + 1
C_ALL = C_ROW + TAB

RSQRT_LINKS = 12
LN1_LINKS = 2 + RSQRT_LINKS
ROPE_LINKS = 3
MID_LINKS = 2 + 1 + RSQRT_LINKS + 1 + 1 + 1 + RSQRT_LINKS + 1
ROUTE_LINKS = 15


def hold(eng, sem, value, passed):
    eng.wait_ge(sem, value)
    eng.sem_inc(passed, 1)


class Chain:

    def __init__(self, eng, sem, done, links, passed=None):
        self.eng, self.sem, self.done, self.links, self.n, self.passed = eng, sem, done, links, 0, passed

    def __call__(self, ins, own=False):
        self.n += 1
        ins.then_inc(self.sem, 1)
        self.eng.wait_ge(self.sem, self.done * self.links + self.n)
        if own:
            self.eng.sem_inc(self.passed, 1)

    def end(self):
        assert self.n == self.links, (self.n, self.links)


def rsqrt(ch, out, var, work):
    dve = ch.eng
    v, y, t = work
    ch(dve.tensor_scalar(v, var, EPS, None, ALU.add))
    ch(dve.tensor_scalar(t.bitcast(U32), v.bitcast(U32), 1, None, ALU.logical_shift_right))
    ch(dve.tensor_scalar(y.bitcast(I32), t.bitcast(I32), -1.0, RSQRT_MAGIC, ALU.mult, ALU.add))
    for n in range(3):
        ch(dve.tensor_tensor(t, y, y, ALU.mult))
        ch(dve.scalar_tensor_tensor(out=t, in0=t, scalar=-0.5, in1=v, op0=ALU.mult, op1=ALU.mult))
        ch(dve.scalar_tensor_tensor(out=y if n < 2 else out, in0=t, scalar=1.5, in1=y,
                                    op0=ALU.add, op1=ALU.mult))


def build(nc, x_in, wqT, wkT, fc1_w, fc1_b, fc2_wT, fc2_b, gate_w, gate_b, w1, b1T, w2, b2,
          cos_t, sin_t, ident_c, mask_c, tri_c, out):
    x_rows = x_in.rearrange("b l d -> (b l) d")
    out_rows = out.rearrange("b l d -> (b l) d")
    sorted_x = nc.dram_tensor("sorted_x", [NE * REGION, XW], F32).ap()
    pair_y = nc.dram_tensor("pair_y", [2 * NT, D], F32).ap()

    with ExitStack() as ctx:
        def sb(name, shape, dt, c=ctx):
            return c.enter_context(nc.sbuf_tensor(name, shape, dt))

        def sem(name, c=ctx):
            return c.enter_context(nc.semaphore(name))

        x_all = sb("x_all", [P, TT, D], F32)
        ident = sb("ident", [P, P], F32)
        b2_all = sb("b2_all", [P, NE, D], F32)
        b1_all = sb("b1_all", [P, NE, FC], F32)
        iota_e = sb("iota_e", [P, NE], F32)
        steer = sb("steer", [1, C_ALL], I32)
        w_stage = [sb(f"w_stage{i}", [P, 2, FC * D], F32) for i in range(2)]
        w_hi = [sb("w_hi0", [P, 2, FC * D], F32R), None]
        w_lo = [sb("w_lo0", [P, 2, FC * D], F32R), None]
        weights_in = [sem(f"weights_in{i}") for i in range(2)]
        w_hi_ready = sem("w_hi_ready")
        w_split = [sem("w1_split"), sem("w2_split")]
        passed = sem("passed")

        def load_weights(sp, e, par):
            sp.dma_start(w_stage[par][:, 0, :].rearrange("p (k f) -> p k f", k=KC),
                         w1[bass.ds(e, 1), :, :].rearrange("e (k p) f -> p (e k) f", p=P)).then_inc(weights_in[par], 16)
            sp.dma_start(w_stage[par][:, 1, :].rearrange("p (c d) -> p c d", c=FC),
                         w2[bass.ds(e, 1), :, :].rearrange("e (c p) d -> p (e c) d", p=P)).then_inc(weights_in[par], 16)

        def round_weights(act, e, par, loads):
            act.wait_ge(weights_in[par], loads * 32)
            for i in range(2):
                act.activation(w_hi[par][:, i, :], w_stage[par][:, i, :], ACT.Copy).then_inc(w_hi_ready, 1)

        def split_weights(pool, e, par):
            for i in range(2):
                pool.wait_ge(w_hi_ready, e * 2 + i + 1)
                pool.tensor_tensor(w_lo[par][:, i, :], w_stage[par][:, i, :],
                                   w_hi[par][:, i, :].bitcast(F32), ALU.subtract).then_inc(w_split[i], 1)

        with ExitStack() as actx:
            def sa(name, shape, dt):
                return sb(name, shape, dt, actx)

            def pa(name, shape, dt):
                return actx.enter_context(nc.psum_tensor(name, shape, dt))

            def sm(name):
                return sem(name, actx)

            wqk = sa("wqk", [P, KC, 2, D], F32)
            wqk_hi = sa("wqk_hi", [P, KC, 2, D], F32R)
            wqk_lo = sa("wqk_lo", [P, KC, 2, D], F32R)
            cos_sb = sa("cos_sb", [P, L], BF16)
            sin_sb = sa("sin_sb", [P, L], BF16)
            identb = sa("identb", [P, P], BF16)
            mask = sa("mask", [P, P], BF16)
            tri = sa("tri", [P, P], BF16)
            ones = sa("ones", [P, P], BF16)
            fc1w = sa("fc1w", [P, INNER], F32)
            fc1b = sa("fc1b", [P, INNER], F32)
            fc2a = sa("fc2a", [P, D], F32)
            gatew = sa("gatew", [P, KC, NE], F32)
            gateb = sa("gateb", [P, NE], F32)
            ids_i = sa("ids_i", [P, TT], I32)
            ids = sa("ids", [P, TT], F32)
            iota_i = sa("iota_i", [P, NE], I32)
            giota_i = sa("giota_i", [1, TAB], I32)
            giota = sa("giota", [1, TAB], F32)
            fill = sa("fill", [P, TM // P, XW], F32)

            stats = sa("stats", [P, TB, 6], F32)
            mv = sa("mv", [P, TB, 2], F32)
            rstd = sa("rstd", [P, TB], F32)
            shift = sa("shift", [P, TB], F32)
            nwork = sa("nwork", [P, 3, TB], F32)
            xn = sa("xn", [P, TB, D], F32)
            xT_hi = sa("xT_hi", [P, KC, L], F32R)
            xT_lo = sa("xT_lo", [P, KC, L], F32R)
            qk = sa("qk", [P, 2, KC, L], BF16)
            rope_a = sa("rope_a", [P, 2, L], BF16)
            rope_b = sa("rope_b", [P, 2, L], BF16)
            qkr = sa("qkr", [P, 2, KC, L], BF16)
            probs = sa("probs", [P, L], BF16)
            osum = sa("osum", [P, TB], F32)
            hid = sa("hid", [P, TB, HID], F32)
            hidT = sa("hidT", [P, 2, P], F32)
            attn = sa("attn", [P, TB, D], F32)
            mstats = sa("mstats", [P, TB, 6], F32)
            mmv = sa("mmv", [P, TB, 2], F32)
            mrstd = sa("mrstd", [P, 2, TB], F32)
            mshift = sa("mshift", [P, 2, TB], F32)
            mwork = sa("mwork", [P, 3, TB], F32)
            xrow = sa("xrow", [P, TB, XW], F32)
            x3T = sa("x3T", [P, KC, L], F32)
            logits = sa("logits", [P, TB, NE], F32)
            top8 = sa("top8", [P, TB, 8], F32)
            idx8 = sa("idx8", [P, TB, 8], U32)
            idxf = sa("idxf", [P, 2, TB], F32)
            onehot = sa("onehot", [P, 2, TB, NE], F32)
            chosen = sa("chosen", [P, TB, NE], BF16)
            scan_in = sa("scan_in", [P, NE, TB + 1], F32)
            scan_keep = sa("scan_keep", [P, NE, TB + 1], F32)
            carry = sa("carry", [P, NE, TB + 1], F32)
            pos = sa("pos", [P, TB, NE], F32)
            slot_w = sa("slot_w", [P, 2, TB, NE], F32)
            slot = sa("slot", [P, 2 * TB], F32)
            slot_i = sa("slot_i", [P, 2 * TB], I32)
            gdiff = sa("gdiff", [P, TB], F32)
            gexp = sa("gexp", [P, TB], F32)
            gden = sa("gden", [P, TB], F32)
            cnt = sa("cnt", [1, 6, NE + 1], F32)
            cnt_i = sa("cnt_i", [1, 2, NE], I32)
            gm = attn[0:1].rearrange("p t d -> p (t d)")[:, 0:3 * TAB * NE].rearrange("p (i n) -> p i n", i=3)

            pT = pa("pT", [P, 2, 512], F32)
            pP = pa("pP", [P, 2, 512], F32)
            pS = pa("pS", [P, 4, 512], F32)
            pA = pS[:, :, :].rearrange("p b (u d) -> p (b u) d", d=D)
            pLog = pP[:, 0, 0:TB * NE]
            pRank = pP[:, 1, 0:TB * NE]
            pTot = pP[:, 1, TB * NE:2 * TB * NE]

            x_first = sm("x_first")
            x_rest = sm("x_rest")
            wqk_in = sm("wqk_in")
            consts_in = sm("consts_in")
            b2_in = sm("b2_in")
            tables_in = sm("tables_in")
            pool_set = sm("pool_set")
            set_up = sm("set_up")
            ln1_link = sm("ln1_link")
            xn_ready = sm("xn_ready")
            xn_turned = sm("xn_turned")
            xT_hi_ready = sm("xT_hi_ready")
            xT_ready = sm("xT_ready")
            projected = sm("projected")
            qk_ready = sm("qk_ready")
            rope_link = sm("rope_link")
            roped = sm("roped")
            scored = sm("scored")
            summed = sm("summed")
            mid_link = sm("mid_link")
            hid_ready = sm("hid_ready")
            hid_turned = sm("hid_turned")
            hidT_ready = sm("hidT_ready")
            mlp_done = sm("mlp_done")
            attn_stats = sm("attn_stats")
            attn_normed = sm("attn_normed")
            x3_stats = sm("x3_stats")
            x3_ready = sm("x3_ready")
            x3_turned = sm("x3_turned")
            x3T_ready = sm("x3T_ready")
            logits_done = sm("logits_done")
            route_link = sm("route_link")
            gdiff_ready = sm("gdiff_ready")
            gexp_ready = sm("gexp_ready")
            chosen_ready = sm("chosen_ready")
            ranked = sm("ranked")
            ranks_read = sm("ranks_read")
            rows_ready = sm("rows_ready")
            rows_sent = sm("rows_sent")
            rows_left = sm("rows_left")
            steer_link = sm("steer_link")
            steer_ready = sm("steer_ready")
            ends_filled = sm("ends_filled")

            CONSTS = 6 + 8
            with nc.Block() as block:

                @block.sync
                def _(sp):
                    sp.dma_start(x_all[:, 0:TB, :], x_rows[0:L, :].rearrange("(t p) d -> p t d", p=P)).then_inc(x_first, 16)
                    for i, w in enumerate((wqT, wkT)):
                        sp.dma_start(wqk[:, :, i, :], w.rearrange("(k p) d -> p k d", p=P)).then_inc(wqk_in, 16)
                    for dst, src in ((ident[:], ident_c),
                                     (fc1w[:], fc1_w.rearrange("i o -> o i").to_broadcast([P, INNER])),
                                     (fc1b[:], fc1_b.rearrange("(o i) -> o i", o=1).to_broadcast([P, INNER])),
                                     (gatew[:], gate_w.rearrange("(k p) e -> p k e", p=P)),
                                     (gateb[:], gate_b.rearrange("(o e) -> o e", o=1).to_broadcast([P, NE])),
                                     (b1_all[:], b1T)):
                        sp.dma_start(dst, src).then_inc(consts_in, 16)
                    for j in range(4):
                        sp.dma_start(fc2a[HID * j:HID * j + INNER, :], fc2_wT).then_inc(consts_in, 16)
                        sp.dma_start(fc2a[HID * j + INNER:HID * j + INNER + 1, :],
                                     fc2_b.rearrange("(o d) -> o d", o=1)).then_inc(consts_in, 16)
                    for b in range(1, B):
                        sp.dma_start(x_all[:, b * TB:(b + 1) * TB, :],
                                     x_rows[b * L:(b + 1) * L, :].rearrange("(t p) d -> p t d", p=P)).then_inc(x_rest, 16)
                    sp.dma_start(b2_all[:].rearrange("p e d -> p (e d)"),
                                 b2.rearrange("e d -> (e d)").rearrange("(o n) -> o n", o=1).to_broadcast([P, NE * D])
                                 ).then_inc(b2_in, 16)
                    for e in range(2):
                        load_weights(sp, e, e)
                    sp.wait_ge(pool_set, 8)
                    sp.wait_ge(steer_ready, 1)
                    for e in range(NE):
                        end = sp.value_load(steer[0:1, C_END + e:C_END + e + 1], min_val=e * REGION,
                                            max_val=e * REGION + NT)
                        sp.dma_start(sorted_x[bass.ds(end, TM), :].rearrange("(a p) c -> p a c", p=P),
                                     fill[:]).then_inc(ends_filled, 16)
                    sp.wait_ge(ends_filled, 16 * NE)
                    sp.wait_ge(b2_in, 16)

                @block.gpsimd
                def _(pool):
                    pool.sem_inc(rows_left, ONE)
                    for dst, src in ((cos_sb, cos_t), (sin_sb, sin_t), (mask, mask_c), (tri, tri_c)):
                        pool.dma_start(dst[:], src).then_inc(tables_in, 16)
                    pool.memset(ones[:], 1.0).then_inc(pool_set, 1)
                    pool.memset(hid[:], 0.0).then_inc(pool_set, 1)
                    pool.memset(fill[:], 0.0).then_inc(pool_set, 1)
                    pool.iota(ids_i[:], pattern=[[P, TT]], base=0, channel_multiplier=1).then_inc(pool_set, 1)
                    pool.iota(iota_i[:], pattern=[[1, NE]], base=0, channel_multiplier=0).then_inc(pool_set, 1)
                    pool.iota(giota_i[:], pattern=[[1, TAB]], base=0, channel_multiplier=0).then_inc(pool_set, 1)
                    pool.wait_ge(pool_set, 6)
                    pool.memset(fill[:, :, D:D + 1], NO_TOKEN).then_inc(pool_set, 1)
                    pool.memset(fill[:, :, D + 1:D + 2], -1.0).then_inc(pool_set, 1)
                    split_weights(pool, 0, 0)

                    with pool.Fori(0, B) as b:
                        hold(pool, rows_ready, b + 1, passed)
                        for i in range(2 * TB):
                            pool.indirect_dma_start(
                                out=sorted_x, out_offset=bass.IndirectOffsetOnAxis(ap=slot_i[:, i:i + 1], axis=0),
                                in_=xrow[:, i % TB, :], in_offset=None).then_inc(rows_sent, 16)
                        hold(pool, rows_sent, (b + 1) * (2 * TB * 16), rows_left)

                @block.scalar
                def _(act):
                    act.sem_inc(attn_normed, ONE)
                    act.sem_inc(gexp_ready, ONE)
                    def turn_hi(b):
                        act.wait_ge(projected, b * 8)
                        for n in range(2 * KC):
                            h, k = n // KC, n % KC
                            act.wait_ge(xn_turned, b * 4 + n + 1)
                            act.activation(xT_hi[:, k, h * 512:(h + 1) * 512], pT[:, n % 2, :],
                                           ACT.Copy).then_inc(xT_hi_ready, 1)

                    def take_qk(b, roped_before):
                        act.wait_ge(roped, roped_before)
                        for n in range(8):
                            h, i, m = n // 4, (n // 2) % 2, n % 2
                            act.wait_ge(projected, b * 8 + n + 1)
                            act.activation(qk[:, i, m, h * 512:(h + 1) * 512], pP[:, n % 2, :],
                                           ACT.Copy).then_inc(qk_ready, 1)

                    def sum_exps(c):
                        act.wait_ge(hid_ready, c + ONE)
                        for t in range(TB):
                            act.wait_ge(scored, c * TB + t + 1)
                            act.wait_ge(summed, c * TB + t)
                            n = (t + 1) * P
                            act.activation(probs[:, 0:n],
                                           pS[:, 2 * (t % 2):2 * (t % 2) + 2, :].rearrange("p b n -> p (b n)")[:, 0:n],
                                           ACT.Exp, scale=1.0 / D ** 0.5,
                                           accum_out=osum[:, t:t + 1]).then_inc(summed, 1)

                    def mlp_and_norm(c):
                        act.wait_ge(hid_turned, c + 1 + ONE)
                        act.activation(hidT[:].rearrange("p g n -> p (g n)"), pT[:, 0, 0:2 * P],
                                       ACT.Copy).then_inc(hidT_ready, 1)
                        act.wait_ge(attn_stats, c + 1)
                        for t in range(TB):
                            act.activation(attn[:, t, :], pA[:, 2 * (t % 4) + t // 4, :], ACT.Identity, bias=mshift[:, 0, t:t + 1],
                                           scale=mrstd[:, 0, t:t + 1]).then_inc(attn_normed, 1)

                    def norm_x3(c):
                        act.wait_ge(x3_stats, c + 1)
                        act.wait_ge(rows_left, c + ONE)
                        for t in range(TB):
                            act.activation(xrow[:, t, 0:D], x_all[:, c * TB + t, :], ACT.Identity,
                                           bias=mshift[:, 1, t:t + 1],
                                           scale=mrstd[:, 1, t:t + 1]).then_inc(x3_ready, 1)
                        for n in range(2 * KC):
                            h, k = n // KC, n % KC
                            act.wait_ge(x3_turned, c * 4 + n + 1)
                            act.activation(x3T[:, k, h * 512:(h + 1) * 512], pT[:, n % 2, :],
                                           ACT.Copy).then_inc(x3T_ready, 1)
                        act.wait_ge(gdiff_ready, c + 1)
                        act.activation(gexp[:], gdiff[:], ACT.Exp).then_inc(gexp_ready, 1)

                    turn_hi(0)
                    take_qk(0, 0)
                    round_weights(act, 0, 0, 1)
                    with act.Fori(0, B - 1) as j:
                        turn_hi(j + 1)
                        sum_exps(j)
                        mlp_and_norm(j)
                        take_qk(j + 1, j + 1)
                        norm_x3(j)
                    sum_exps(B - 1)
                    mlp_and_norm(B - 1)
                    norm_x3(B - 1)

                @block.tensor
                def _(pe):
                    pe.sem_inc(hid_turned, ONE)
                    def turn_x(b):
                        for n in range(2 * KC):
                            h, k = n // KC, n % KC
                            if n >= 2:
                                pe.wait_ge(xT_ready, b * 4 + n - 1)
                            for u in range(4):
                                t = 4 * h + u
                                if k == 0:
                                    pe.wait_ge(xn_ready, b * TB + t + 1)
                                mm = pe.transpose(pT[:, n % 2, u * P:(u + 1) * P], xn[:, t, k * P:(k + 1) * P], ident[:])
                            mm.then_inc(xn_turned, 1)

                    def project(b, routed):
                        pe.wait_ge(ranks_read, routed + ONE)
                        for n in range(8):
                            h, i, m = n // 4, (n // 2) % 2, n % 2
                            pe.wait_ge(xT_ready, b * 4 + 2 * (h + 1))
                            if n >= 2:
                                pe.wait_ge(qk_ready, b * 8 + n - 1)
                            tok = slice(h * 512, (h + 1) * 512)
                            mo = slice(m * P, (m + 1) * P)
                            for k in range(KC):
                                for w, x in ((wqk_lo, xT_hi), (wqk_hi, xT_hi), (wqk_hi, xT_lo)):
                                    mm = pe.matmul(pP[:, n % 2, :], w[:, k, i, mo], x[:, k, tok],
                                                   start=(k == 0 and w is wqk_lo), stop=(k == KC - 1 and x is xT_lo))
                            mm.then_inc(projected, 1)

                    def score(c):
                        pe.wait_ge(roped, c + 1)
                        pe.wait_ge(attn_normed, c * TB + ONE)
                        for t in range(TB):
                            if t >= 2:
                                pe.wait_ge(summed, c * TB + t - 1)
                            keys = (t + 1) * P
                            for a in range(0, keys, 512):
                                n = min(512, keys - a)
                                bank = pS[:, 2 * (t % 2) + a // 512, :]
                                last = a + n == keys
                                for m in range(KC):
                                    mm = pe.matmul(bank[:, 0:n], qkr[:, 0, m, t * P:(t + 1) * P],
                                                   qkr[:, 1, m, a:a + n], start=(m == 0), stop=(m == KC - 1 and not last))
                                if last:
                                    mm = pe.matmul(bank[:, n - P:n], identb[:], mask[:], start=False, stop=True)
                            mm.then_inc(scored, 1)

                    def attention_mlp(c, fronts):
                        pe.wait_ge(hid_ready, c + 1 + ONE)
                        pe.wait_ge(xT_ready, fronts * 4)
                        for g in range(2):
                            mm = pe.transpose(pT[:, 0, g * P:(g + 1) * P],
                                              hid[:, 4 * g:4 * g + 4, :].rearrange("p t h -> p (t h)"), ident[:])
                        mm.then_inc(hid_turned, 1)
                        pe.wait_ge(hidT_ready, c + 1)
                        pe.wait_ge(summed, (c + 1) * TB)
                        for j in range(4):
                            rows = slice(HID * j, HID * j + INNER + 1)
                            for g in range(2):
                                mm = pe.matmul(pA[:, 2 * j + g, :], hidT[rows, g, :], fc2a[rows, :],
                                               start=True, stop=True)
                            mm.then_inc(mlp_done, 1)

                    def gate(c, fronts):
                        for n in range(2 * KC):
                            h, k = n // KC, n % KC
                            if n >= 2:
                                pe.wait_ge(x3T_ready, c * 4 + n - 1)
                            for u in range(4):
                                t = 4 * h + u
                                if k == 0:
                                    pe.wait_ge(x3_ready, c * TB + t + 1)
                                mm = pe.transpose(pT[:, n % 2, u * P:(u + 1) * P], xrow[:, t, k * P:(k + 1) * P], ident[:])
                            mm.then_inc(x3_turned, 1)
                        pe.wait_ge(x3T_ready, (c + 1) * 4)
                        pe.wait_ge(qk_ready, fronts * 8)
                        for t in range(TB):
                            for k in range(KC):
                                mm = pe.matmul(pLog[:, t * NE:(t + 1) * NE], x3T[:, k, t * P:(t + 1) * P],
                                               gatew[:, k, :], start=(k == 0), stop=(k == KC - 1))
                        mm.then_inc(logits_done, 1)
                        pe.wait_ge(chosen_ready, c + 1)
                        ch = chosen[:].rearrange("p t e -> p (t e)")
                        pe.matmul(pRank, tri[:], ch, start=True, stop=True)
                        pe.matmul(pTot, ones[:], ch, start=True, stop=True).then_inc(ranked, 1)

                    pe.wait_ge(tables_in, 64)
                    pe.wait_ge(consts_in, 16 * CONSTS)
                    pe.wait_ge(set_up, 4)
                    turn_x(0)
                    project(0, 0)
                    with pe.Fori(0, B - 1) as j:
                        turn_x(j + 1)
                        score(j)
                        attention_mlp(j, j + 2)
                        project(j + 1, j)
                        gate(j, j + 2)
                    score(B - 1)
                    attention_mlp(B - 1, B)
                    gate(B - 1, B)

                @block.vector
                def _(dve):
                    dve.sem_inc(hid_ready, ONE)
                    dve.sem_inc(ranks_read, ONE)
                    def norm_x(b):
                        ch = Chain(dve, ln1_link, b, LN1_LINKS, passed)
                        for t in range(TB):
                            s = dve.bn_stats(stats[:, t, :], x_all[:, b * TB + t, :])
                        ch(s, own=True)
                        for t in range(TB):
                            s = dve.bn_aggr(mv[:, t, :], stats[:, t, :])
                        ch(s)
                        rsqrt(ch, rstd[:], mv[:, :, 1], [nwork[:, i, :] for i in range(3)])
                        ch.end()
                        dve.wait_ge(xn_turned, b * 4)
                        for t in range(TB):
                            dve.tensor_scalar(xn[:, t, :], x_all[:, b * TB + t, :], mv[:, t, 0:1], rstd[:, t:t + 1],
                                              ALU.subtract, ALU.mult).then_inc(xn_ready, 1)

                    def turn_lo(b):
                        for n in range(2 * KC):
                            h, k = n // KC, n % KC
                            dve.wait_ge(xT_hi_ready, b * 4 + n + 1)
                            tok = slice(h * 512, (h + 1) * 512)
                            dve.tensor_tensor(xT_lo[:, k, tok], pT[:, n % 2, :], xT_hi[:, k, tok].bitcast(F32),
                                              ALU.subtract).then_inc(xT_ready, 1)

                    def rope(b):
                        dve.wait_ge(qk_ready, (b + 1) * 8)
                        dve.wait_ge(scored, b * TB)
                        co = cos_sb[:].rearrange("p (o n) -> p o n", o=1).to_broadcast([P, 2, L])
                        si = sin_sb[:].rearrange("p (o n) -> p o n", o=1).to_broadcast([P, 2, L])
                        ch = Chain(dve, rope_link, b, ROPE_LINKS)
                        for m, op in ((0, ALU.subtract), (1, ALU.add)):
                            dve.tensor_tensor(rope_a[:], qk[:, :, m, :], co, ALU.mult)
                            ch(dve.tensor_tensor(rope_b[:], qk[:, :, 1 - m, :], si, ALU.mult))
                            last = dve.tensor_tensor(qkr[:, :, m, :], rope_a[:], rope_b[:], op)
                            if m == 0:
                                ch(last)
                        ch.end()
                        last.then_inc(roped, 1)

                    def mid(c):
                        ch = Chain(dve, mid_link, c, MID_LINKS, passed)
                        dve.wait_ge(summed, (c + 1) * TB)
                        dve.wait_ge(hid_turned, c + ONE)
                        h16 = hid[:, :, 0:INNER]
                        ch(dve.tensor_tensor(h16, osum[:].rearrange("p (t o) -> p t o", o=1).to_broadcast([P, TB, INNER]),
                                             fc1w[:].rearrange("p (o i) -> p o i", o=1).to_broadcast([P, TB, INNER]),
                                             ALU.mult))
                        ch(dve.tensor_tensor(h16, h16,
                                             fc1b[:].rearrange("p (o i) -> p o i", o=1).to_broadcast([P, TB, INNER]),
                                             ALU.add))
                        dve.tensor_scalar(h16, h16, 0.0, None, ALU.max).then_inc(hid_ready, 1)
                        for j in range(4):
                            dve.wait_ge(mlp_done, c * 4 + j + 1)
                            for g in range(2):
                                s = dve.bn_stats(mstats[:, 4 * g + j, :], pA[:, 2 * j + g, :])
                        ch(s, own=True)

                        def scale_and_shift(i):
                            for t in range(TB):
                                s = dve.bn_aggr(mmv[:, t, :], mstats[:, t, :])
                            return s

                        s = scale_and_shift(0)
                        ch(s)
                        rsqrt(ch, mrstd[:, 0, :], mmv[:, :, 1], [mwork[:, i, :] for i in range(3)])
                        dve.scalar_tensor_tensor(out=mshift[:, 0, :], in0=mmv[:, :, 0], scalar=-1.0, in1=mrstd[:, 0, :],
                                                 op0=ALU.mult, op1=ALU.mult).then_inc(attn_stats, 1)
                        dve.wait_ge(attn_normed, (c + 1) * TB + ONE)
                        xb = x_all[:, bass.ds(c * TB, TB), :]
                        ch(dve.tensor_tensor(xb, xb, attn[:], ALU.add), own=True)
                        for t in range(TB):
                            s = dve.bn_stats(mstats[:, t, :], x_all[:, c * TB + t, :])
                        ch(s, own=True)
                        ch(scale_and_shift(1))
                        rsqrt(ch, mrstd[:, 1, :], mmv[:, :, 1], [mwork[:, i, :] for i in range(3)])
                        dve.scalar_tensor_tensor(out=mshift[:, 1, :], in0=mmv[:, :, 0], scalar=-1.0, in1=mrstd[:, 1, :],
                                                 op0=ALU.mult, op1=ALU.mult).then_inc(x3_stats, 1)
                        ch.end()

                    def route(c):
                        ch = Chain(dve, route_link, c, ROUTE_LINKS, passed)
                        dve.wait_ge(logits_done, c + 1)
                        ch(dve.tensor_tensor(logits[:], pLog.rearrange("p (t e) -> p t e", e=NE),
                                             gateb[:].rearrange("p (o e) -> p o e", o=1).to_broadcast([P, TB, NE]), ALU.add),
                           own=True)
                        for t in range(TB):
                            s = dve.max(top8[:, t, :], logits[:, t, :])
                        ch(s, own=True)
                        for t in range(TB):
                            s = dve.max_index(idx8[:, t, :], top8[:, t, :], logits[:, t, :])
                        ch(s)
                        dve.wait_ge(gexp_ready, c + ONE)
                        dve.tensor_tensor(gdiff[:], top8[:, :, 1], top8[:, :, 0], ALU.subtract).then_inc(gdiff_ready, 1)
                        ch(dve.tensor_copy(idxf[:], idx8[:, :, 0:2].rearrange("p t k -> p k t")))
                        io = iota_e[:].rearrange("p (o e) -> p o e", o=1).to_broadcast([P, TB, NE])
                        for k in range(2):
                            s = dve.tensor_tensor(onehot[:, k], io,
                                                  idxf[:, k, :].rearrange("p (t o) -> p t o", o=1).to_broadcast([P, TB, NE]),
                                                  ALU.is_equal)
                        ch(s)
                        dve.tensor_tensor(chosen[:], onehot[:, 0], onehot[:, 1], ALU.add).then_inc(chosen_ready, 1)
                        dve.wait_ge(ranked, c + 1)
                        ch(dve.tensor_copy(scan_in[:, :, 1:TB + 1], pTot.rearrange("p (t e) -> p e t", e=NE)))
                        ch(dve.tensor_tensor_scan(carry[:].rearrange("p e t -> p (e t)"),
                                                  scan_keep[:].rearrange("p e t -> p (e t)"),
                                                  scan_in[:].rearrange("p e t -> p (e t)"), 0.0, ALU.mult, ALU.add))
                        dve.tensor_tensor(pos[:], pRank.rearrange("p (t e) -> p t e", e=NE),
                                          carry[:, :, 0:TB].rearrange("p e t -> p t e"), ALU.add).then_inc(ranks_read, 1)
                        ch(dve.tensor_copy(scan_in[:, :, 0:1], carry[:, :, TB:TB + 1]))
                        dve.wait_ge(ranks_read, c + 1 + ONE)
                        for k in range(2):
                            s = dve.tensor_tensor(slot_w[:, k], onehot[:, k], pos[:], ALU.mult)
                        ch(s)
                        ch(dve.tensor_reduce(slot[:], slot_w[:].rearrange("p k t e -> p (k t) e"), AX_X, ALU.add))
                        dve.wait_ge(rows_left, c + ONE)
                        ch(dve.tensor_copy(slot_i[:], slot[:]))
                        dve.wait_ge(x3_ready, (c + 1) * TB)
                        ch(dve.tensor_copy(xrow[:, :, D], ids[:, bass.ds(c * TB, TB)]))
                        ch(dve.tensor_copy(xrow[:, :, D + 1], idxf[:, 0, :]))
                        dve.wait_ge(gexp_ready, c + 1 + ONE)
                        ch(dve.tensor_scalar(gden[:], gexp[:], 1.0, None, ALU.add))
                        ch(dve.reciprocal(xrow[:, :, D + 2], gden[:]))
                        dve.tensor_tensor(xrow[:, :, D + 3], gexp[:], xrow[:, :, D + 2],
                                          ALU.mult).then_inc(rows_ready, 1)
                        ch.end()

                    def steer_table():
                        n = [0]

                        def ch(ins):
                            n[0] += 1
                            ins.then_inc(steer_link, 1)
                            dve.wait_ge(steer_link, n[0])

                        end, count, tiles, incl, base, keep = (cnt[:, i, 0:NE] for i in range(6))
                        ch(dve.tensor_copy(end, carry[0:1, :, TB]))
                        ch(dve.scalar_tensor_tensor(out=count, in0=iota_e[0:1, :], scalar=-float(REGION), in1=end,
                                                    op0=ALU.mult, op1=ALU.add))
                        ch(dve.tensor_scalar(cnt_i[:, 0, :], count, float(TM - 1), None, ALU.add))
                        ch(dve.tensor_scalar(cnt_i[:, 1, :], cnt_i[:, 0, :], int(np.log2(TM)), None,
                                             ALU.arith_shift_right))
                        ch(dve.tensor_copy(tiles, cnt_i[:, 1, :]))
                        ch(dve.memset(keep, 1.0))
                        ch(dve.tensor_tensor_scan(incl, keep, tiles, 0.0, ALU.mult, ALU.add))
                        ch(dve.tensor_tensor(base, incl, tiles, ALU.subtract))
                        for at, v in ((C_END, end), (C_TILES, tiles), (C_BASE, base)):
                            ch(dve.tensor_copy(steer[:, at:at + NE], v))
                        G = TAB
                        a, w, r = (gm[:, i, :].rearrange("o (g e) -> o g e", e=NE) for i in range(3))
                        gi = giota[:].rearrange("o (g u) -> o g u", u=1).to_broadcast([1, G, NE])

                        def per_e(v):
                            return v.rearrange("o (u e) -> o u e", u=1).to_broadcast([1, G, NE])

                        ch(dve.tensor_tensor(a, gi, per_e(base), ALU.is_ge))
                        ch(dve.tensor_tensor(w, gi, per_e(incl), ALU.is_lt))
                        ch(dve.tensor_tensor(a, a, w, ALU.mult))
                        ch(dve.tensor_tensor(w, gi, per_e(base), ALU.subtract))
                        ch(dve.tensor_scalar(w, w, float(TM), None, ALU.mult))
                        ch(dve.scalar_tensor_tensor(out=r, in0=per_e(iota_e[0:1, :]), scalar=float(REGION), in1=w,
                                                    op0=ALU.mult, op1=ALU.add))
                        ch(dve.tensor_tensor(r, r, a, ALU.mult))
                        ch(dve.tensor_reduce(gm[:, 1, 0:G], r, AX_X, ALU.add))
                        ch(dve.tensor_reduce(gm[:, 2, 0:G], a, AX_X, ALU.add))
                        ch(dve.tensor_scalar(gm[:, 2, 0:G], gm[:, 2, 0:G], -1.0, 1.0, ALU.mult, ALU.add))
                        ch(dve.scalar_tensor_tensor(out=gm[:, 1, 0:G], in0=gm[:, 2, 0:G], scalar=end[:, 0:1],
                                                    in1=gm[:, 1, 0:G], op0=ALU.mult, op1=ALU.add))
                        dve.tensor_copy(steer[:, C_ROW:C_ROW + G], gm[:, 1, 0:G]).then_inc(steer_ready, 1)

                    dve.wait_ge(wqk_in, 32)
                    dve.tensor_copy(wqk_hi[:], wqk[:]).then_inc(set_up, 1)
                    dve.wait_ge(set_up, 1)
                    dve.tensor_tensor(wqk_lo[:], wqk[:], wqk_hi[:].bitcast(F32), ALU.subtract).then_inc(set_up, 1)
                    dve.wait_ge(pool_set, 8)
                    dve.tensor_scalar(hid[:, :, INNER], hid[:, :, INNER + 1], 1.0, None, ALU.add)
                    dve.tensor_copy(ids[:], ids_i[:])
                    dve.tensor_copy(giota[:], giota_i[:])
                    dve.memset(scan_keep[:], 1.0)
                    dve.tensor_copy(iota_e[:], iota_i[:]).then_inc(set_up, 1)
                    dve.wait_ge(set_up, 3)
                    dve.tensor_scalar(scan_in[:, :, 0], iota_e[:], float(REGION), None, ALU.mult)
                    dve.memset(scan_keep[:, :, 0:1], 0.0)
                    dve.wait_ge(tables_in, 64)
                    dve.wait_ge(consts_in, 16 * CONSTS)
                    dve.tensor_copy(identb[:], ident[:]).then_inc(set_up, 1)
                    dve.wait_ge(set_up, 4)
                    dve.wait_ge(x_first, 16)
                    norm_x(0)
                    turn_lo(0)
                    rope(0)
                    dve.wait_ge(x_rest, 16 * (B - 1))
                    with dve.Fori(0, B - 1) as j:
                        norm_x(j + 1)
                        turn_lo(j + 1)
                        mid(j)
                        rope(j + 1)
                        route(j)
                    mid(B - 1)
                    route(B - 1)
                    steer_table()

        with ExitStack() as ectx:
            def se(name, shape, dt):
                return sb(name, shape, dt, ectx)

            def pe_sum(name, shape, dt):
                return ectx.enter_context(nc.psum_tensor(name, shape, dt))

            def sm(name):
                return sem(name, ectx)

            w_hi[1] = se("w_hi1", [P, 2, FC * D], F32R)
            w_lo[1] = se("w_lo1", [P, 2, FC * D], F32R)
            xt = se("xt", [P, TM // P, XW], F32)
            xeT_hi = se("xeT_hi", [P, KC, TM], F32R)
            xeT_lo = se("xeT_lo", [P, KC, TM], F32R)
            h = se("h", [P, FC, TM], F32)
            h_hi = se("h_hi", [P, FC, TM], F32R)
            h_lo = se("h_lo", [P, FC, TM], F32R)
            tag = se("tag", [P, TM // P, 4], F32)
            other = se("other", [P, TM // P], F32)
            same = se("same", [P, TM // P], F32)
            wa = se("wa", [P, TM // P], F32)
            wb = se("wb", [P, TM // P], F32)
            weight = se("weight", [P, TM // P], F32)
            dest = se("dest", [P, TM // P], I32)
            y = se("y", [P, TM // P, D], F32)
            pL = pe_sum("pL", [P, 4, 512], F32)
            pX = pe_sum("pX", [P, KC, TM], F32)
            pY = pe_sum("pY", [P, 2, 512], F32)

            tile_in = sm("tile_in")
            tile_turned = sm("tile_turned")
            tag_saved = sm("tag_saved")
            xeT_hi_ready = sm("xeT_hi_ready")
            xeT_ready = sm("xeT_ready")
            l1_done = sm("l1_done")
            h_ready = sm("h_ready")
            h_hi_ready = sm("h_hi_ready")
            h_split = sm("h_split")
            l2_done = sm("l2_done")
            tag_link = sm("tag_link")
            y_added = sm("y_added")
            y_ready = sm("y_ready")
            y_sent = sm("y_sent")
            y_left = sm("y_left")
            TAG_LINKS = 5

            def is_last(e):
                return type(e) is int and e == NE - 1

            def over_tiles(eng, start, tile):
                def expert(pair, par):
                    e = pair * 2 + par
                    n = eng.value_load(steer[0:1, bass.ds(C_TILES + e, 1)], min_val=0, max_val=TPE)
                    base = eng.value_load(steer[0:1, bass.ds(C_BASE + e, 1)], min_val=0, max_val=MAXG)
                    if start:
                        start(e, pair, par, base)
                    with eng.Fori(0, TPE // GRP) as u:
                        with eng.If(u * GRP < n):
                            with eng.Fori(0, GRP) as v:
                                with eng.If(u * GRP + v < n):
                                    tile(e, par, base + u * GRP + v)

                with eng.Fori(0, NE // 2 - 1) as pair:
                    for par in range(2):
                        expert(pair, par)
                for par in range(2):
                    expert(NE // 2 - 1, par)

            with nc.Block() as block:

                @block.sync
                def _(sp):
                    def load_tile(g):
                        row = sp.value_load(steer[0:1, bass.ds(C_ROW + g, 1)], min_val=0, max_val=NE * REGION - TM)
                        sp.dma_start(xt[:], sorted_x[bass.ds(row, TM), :].rearrange("(a p) c -> p a c", p=P)
                                     ).then_inc(tile_in, 16)

                    def start(e, pair, par, base):
                        if type(e) is not int:
                            for i in range(2):
                                sp.wait_ge(w_split[i], e + 1)
                            load_weights(sp, e + 2, par)

                    def tile(e, par, g):
                        sp.wait_ge(tile_turned, g + 1)
                        sp.wait_ge(tag_saved, g + 1)
                        load_tile(g + 1)

                    load_tile(0)
                    over_tiles(sp, start, tile)

                @block.gpsimd
                def _(pool):
                    pool.sem_inc(y_left, ONE)
                    def start(e, pair, par, base):
                        if not is_last(e):
                            pool.wait_ge(l2_done, 2 * base + ONE)
                            split_weights(pool, e + 1, 1 - par)

                    def tile(e, par, g):
                        for i in range(TM // P):
                            hold(pool, y_ready, 2 * g + i + 1, passed)
                            pool.indirect_dma_start(
                                out=pair_y, out_offset=bass.IndirectOffsetOnAxis(ap=dest[:, i:i + 1], axis=0),
                                in_=y[:, i, :], in_offset=None, bounds_check=2 * NT - 1,
                                oob_is_err=False).then_inc(y_sent, 16)
                        hold(pool, y_sent, (g + 1) * 32, y_left)

                    over_tiles(pool, start, tile)

                @block.scalar
                def _(act):
                    def turn_hi(g):
                        act.wait_ge(tile_turned, g + 1)
                        act.activation(xeT_hi[:], pX[:], ACT.Copy).then_inc(xeT_hi_ready, 1)

                    def start(e, pair, par, base):
                        if not is_last(e):
                            act.wait_ge(l2_done, 2 * base + ONE)
                            round_weights(act, e + 1, 1 - par, pair + par + 1)

                    def tile(e, par, g):
                        act.wait_ge(h_split, 4 * g + ONE)
                        for bk in range(4):
                            act.wait_ge(l1_done, 4 * g + bk + 1)
                            for i in range(2):
                                c = 2 * bk + i
                                a = act.activation(h[:, c, :], pL[:, bk, i * TM:(i + 1) * TM], ACT.Gelu,
                                                   bias=b1_all[:, bass.ds(e, 1), c:c + 1].rearrange("p e c -> p (e c)"))
                            a.then_inc(h_ready, 1)
                        turn_hi(g + 1)

                    turn_hi(0)
                    over_tiles(act, start, tile)

                @block.tensor
                def _(pe):
                    pe.sem_inc(l2_done, ONE)
                    def turn(g):
                        pe.wait_ge(tile_in, 16 * (g + 1))
                        for k in range(KC):
                            for i in range(TM // P):
                                mm = pe.transpose(pX[:, k, i * P:(i + 1) * P], xt[:, i, k * P:(k + 1) * P], ident[:])
                        mm.then_inc(tile_turned, 1)

                    def start(e, pair, par, base):
                        hold(pe, w_split[0], e + 1, passed)

                    def tile(e, par, g):
                        hi, lo = w_hi[par], w_lo[par]
                        pe.wait_ge(xeT_ready, g + 1)
                        for bk in range(4):
                            for i in range(2):
                                c = 2 * bk + i
                                for k in range(KC):
                                    col = slice(k * F + c * P, k * F + (c + 1) * P)
                                    for w, x in ((lo, xeT_hi), (hi, xeT_hi), (hi, xeT_lo)):
                                        mm = pe.matmul(pL[:, bk, i * TM:(i + 1) * TM], w[:, 0, col], x[:, k, :],
                                                       start=(k == 0 and w is lo), stop=(k == KC - 1 and x is xeT_lo))
                            mm.then_inc(l1_done, 1)
                        turn(g + 1)
                        pe.wait_ge(w_split[1], e + 1)
                        pe.wait_ge(y_added, 2 * g + ONE)
                        for i in range(TM // P):
                            rows = slice(i * P, (i + 1) * P)
                            for c in range(FC):
                                if i == 0 and c % 2 == 0:
                                    pe.wait_ge(h_split, 4 * g + c // 2 + 1 + ONE)
                                for s, w in ((h_lo, hi), (h_hi, hi), (h_hi, lo)):
                                    mm = pe.matmul(pY[:, i, 0:D], s[:, c, rows], w[:, 1, c * D:(c + 1) * D],
                                                   start=(c == 0 and s is h_lo), stop=(c == FC - 1 and w is lo))
                            mm.then_inc(l2_done, 1)

                    turn(0)
                    over_tiles(pe, start, tile)

                @block.vector
                def _(dve):
                    dve.sem_inc(h_split, ONE)
                    dve.sem_inc(y_added, ONE)
                    def turn_lo(g):
                        dve.wait_ge(xeT_hi_ready, g + 1)
                        dve.tensor_tensor(xeT_lo[:], pX[:], xeT_hi[:].bitcast(F32), ALU.subtract).then_inc(xeT_ready, 1)
                        dve.wait_ge(tile_in, 16 * (g + 1))
                        dve.tensor_copy(tag[:], xt[:, :, D:XW]).then_inc(tag_saved, 1)

                    def tile(e, par, g):
                        dve.wait_ge(l2_done, 2 * g + ONE)
                        for bk in range(4):
                            cs = slice(2 * bk, 2 * bk + 2)
                            dve.wait_ge(h_ready, 4 * g + bk + 1)
                            dve.tensor_copy(h_hi[:, cs, :], h[:, cs, :]).then_inc(h_hi_ready, 1)
                            dve.wait_ge(h_hi_ready, 4 * g + bk + 1)
                            dve.tensor_tensor(h_lo[:, cs, :], h[:, cs, :], h_hi[:, cs, :].bitcast(F32),
                                              ALU.subtract).then_inc(h_split, 1)
                        dve.wait_ge(y_left, g + ONE)
                        dve.wait_ge(tag_saved, g + 1)
                        ch = Chain(dve, tag_link, g, TAG_LINKS)
                        me = iota_e[:, bass.ds(e, 1)]
                        ch(dve.tensor_scalar(same[:], tag[:, :, 1], me, None, ALU.is_equal))
                        ch(dve.tensor_scalar(other[:], same[:], -1.0, 1.0, ALU.mult, ALU.add))
                        ch(dve.scalar_tensor_tensor(out=dest[:], in0=other[:], scalar=float(NT), in1=tag[:, :, 0],
                                                    op0=ALU.mult, op1=ALU.add))
                        dve.tensor_tensor(wa[:], same[:], tag[:, :, 2], ALU.mult)
                        ch(dve.tensor_tensor(wb[:], other[:], tag[:, :, 3], ALU.mult))
                        ch(dve.tensor_tensor(weight[:], wa[:], wb[:], ALU.add))
                        turn_lo(g + 1)
                        for i in range(TM // P):
                            dve.wait_ge(l2_done, 2 * g + i + 1 + ONE)
                            dve.tensor_tensor(y[:, i, :], pY[:, i, 0:D],
                                              b2_all[:, bass.ds(e, 1), :].rearrange("p e d -> p (e d)"),
                                              ALU.add).then_inc(y_added, 1)
                            dve.wait_ge(y_added, 2 * g + i + 1 + ONE)
                            dve.tensor_scalar(y[:, i, :], y[:, i, :], weight[:, i:i + 1], None,
                                              ALU.mult).then_inc(y_ready, 1)
                        ch.end()

                    turn_lo(0)
                    over_tiles(dve, None, tile)

        with ExitStack() as octx:
            def so(name, shape, dt):
                return sb(name, shape, dt, octx)

            def sm(name):
                return sem(name, octx)

            SG = 4
            STEPS = TT // SG
            pair = [so(f"pair{i}", [P, 2, SG, D], F32) for i in range(2)]
            z = [so(f"z{i}", [P, SG, D], F32) for i in range(2)]
            fstats = so("fstats", [P, SG, 6], F32)
            fmv = so("fmv", [P, SG, 2], F32)
            frstd = [so(f"frstd{i}", [P, SG], F32) for i in range(2)]
            fshift = [so(f"fshift{i}", [P, SG], F32) for i in range(2)]
            fwork = so("fwork", [P, 3, SG], F32)
            pair_in = [sm(f"pair_in{i}") for i in range(2)]
            out_link = sm("out_link")
            out_stats = sm("out_stats")
            out_normed = sm("out_normed")
            out_ready = sm("out_ready")
            stored = [sm(f"stored{i}") for i in range(2)]
            OUT_LINKS = 3 + RSQRT_LINKS
            y_tiles = pair_y.rearrange("(k t p) d -> p k t d", k=2, p=P)
            out_tiles = out_rows.rearrange("(t p) d -> p t d", p=P)

            with nc.Block() as block:

                @block.sync
                def _(sp):
                    for u in range(2):
                        sp.sem_inc(stored[u], ONE)
                    def load(s, u):
                        for k in range(2):
                            sp.dma_start(pair[u][:, k], y_tiles[:, k, bass.ds(s * SG, SG), :]).then_inc(pair_in[u], 16)

                    def store(s, u):
                        sp.wait_ge(out_ready, s + 1)
                        sp.dma_start(out_tiles[:, bass.ds(s * SG, SG), :], z[u][:]).then_inc(stored[u], 16)

                    for u in range(2):
                        load(u, u)
                    with sp.Fori(0, STEPS // 2 - 1) as r:
                        for u in range(2):
                            sp.wait_ge(out_normed, (2 * r + u + 1) * SG + ONE)
                            load(2 * r + u + 2, u)
                            store(2 * r + u, u)
                    for u in range(2):
                        store(STEPS - 2 + u, u)
                    for u in range(2):
                        sp.wait_ge(stored[u], 16 * (STEPS // 2) + ONE)

                @block.vector
                def _(dve):
                    with dve.Fori(0, STEPS // 2) as r:
                        for u in range(2):
                            s = 2 * r + u
                            ch = Chain(dve, out_link, s, OUT_LINKS, passed)
                            dve.wait_ge(pair_in[u], 32 * (r + 1))
                            f = pair[u][:, 0]
                            ch(dve.tensor_tensor(f, f, pair[u][:, 1], ALU.add))
                            for t in range(SG):
                                last = dve.bn_stats(fstats[:, t, :], f[:, t, :])
                            ch(last, own=True)
                            for t in range(SG):
                                last = dve.bn_aggr(fmv[:, t, :], fstats[:, t, :])
                            ch(last)
                            dve.wait_ge(out_normed, SG * 2 * r + ONE)
                            rsqrt(ch, frstd[u][:], fmv[:, :, 1], [fwork[:, i, :] for i in range(3)])
                            ch.end()
                            dve.scalar_tensor_tensor(out=fshift[u][:], in0=fmv[:, :, 0], scalar=-1.0, in1=frstd[u][:],
                                                     op0=ALU.mult, op1=ALU.mult).then_inc(out_stats, 1)

                @block.scalar
                def _(act):
                    act.sem_inc(out_normed, ONE)
                    with act.Fori(0, STEPS // 2) as r:
                        for u in range(2):
                            s = 2 * r + u
                            act.wait_ge(out_stats, s + 1)
                            act.wait_ge(stored[u], 16 * r + ONE)
                            for t in range(SG):
                                act.activation(z[u][:, t, :], pair[u][:, 0, t, :], ACT.Identity,
                                               bias=fshift[u][:, t:t + 1],
                                               scale=frstd[u][:, t:t + 1]).then_inc(out_normed, 1)

                @block.gpsimd
                def _(pool):
                    with pool.Fori(0, STEPS // 2) as r:
                        for u in range(2):
                            s = 2 * r + u
                            pool.wait_ge(out_normed, (s + 1) * SG + ONE)
                            pool.tensor_tensor(z[u][:], z[u][:], x_all[:, bass.ds(s * SG, SG), :],
                                               ALU.add).then_inc(out_ready, 1)


def constants():
    inv = np.float32(32.0) ** (-np.arange(0, D, 2, dtype=np.float32) / np.float32(D))
    ang = np.arange(L, dtype=np.float32)[None, :] * inv.astype(np.float32)[:, None]
    row, col = np.arange(P)[:, None], np.arange(P)[None, :]
    return {
        "cos_t": np.cos(ang),
        "sin_t": np.sin(ang),
        "ident_c": (row == col).astype(np.float32),
        "mask_c": np.where(col > row, np.float32(MASKED), np.float32(0.0)),
        "tri_c": (row < col).astype(np.float32),
    }


def kernel(**inputs):
    import concourse.bacc as bacc
    from concourse.bass_utils import run_bass_kernel_spmd

    nc = bacc.Bacc("TRN2", target_bir_lowering=False, num_devices=1)
    g = {k: np.asarray(v) for k, v in inputs.items()}
    arrays = {
        "x": g["L0_attn_hidden_states"],
        "wqT": g["L0_attn_Wq"].T,
        "wkT": g["L0_attn_Wk"].T,
        "fc1_w": g["L0_attn_fc1_w"],
        "fc1_b": g["L0_attn_fc1_b"],
        "fc2_wT": g["L0_attn_fc2_w"].T,
        "fc2_b": g["L0_attn_fc2_b"],
        "gate_w": g["L0_ffn_gate_w"],
        "gate_b": g["L0_ffn_gate_b"],
        "w1": g["L0_ffn_w1"],
        "b1T": g["L0_ffn_b1"].reshape(NE, FC, P).transpose(2, 0, 1),
        "w2": g["L0_ffn_w2"],
        "b2": g["L0_ffn_b2"],
        **constants(),
    }
    arrays = {k: np.ascontiguousarray(v) for k, v in arrays.items()}
    args = [nc.dram_tensor(k, v.shape, mybir.dt.from_np(v.dtype), kind="ExternalInput").ap() for k, v in arrays.items()]
    args.append(nc.dram_tensor("out", [B, L, D], F32, kind="ExternalOutput").ap())
    build(nc, *args)
    r = run_bass_kernel_spmd(nc, [arrays], core_ids=[0])
    return r.results[0]["out"]
```

```python
from contextlib import ExitStack

import numpy as np
import concourse.bass as bass
from concourse import mybir

F32 = mybir.dt.float32
F32R = mybir.dt.float32r
BF16 = mybir.dt.bfloat16
I32 = mybir.dt.int32
U32 = mybir.dt.uint32
ALU = mybir.AluOpType
ACT = mybir.ActivationFunctionType
AX_X = mybir.AxisListType.X

P = 128
EPS = 1e-5
RSQRT_MAGIC = float(0x5F3759DF)
MASKED = -1e30

B, L, D = 4, 1024, 256
NT = B * L
KC = D // P
TB = L // P
TT = NT // P
INNER = 16
HK = INNER + 1
HID = 64
NE, F = 8, 1024
FC = F // P
TM = 256
TPE = NT // TM
MAXG = 2 * NT // TM + NE
REGION = NT + TM
XW = D + 4
NO_TOKEN = 4.0 * NT

ONE = 1

C_END, C_TILES, C_BASE, C_ROW = 0, NE, 2 * NE, 3 * NE
TAB = MAXG + 2 * TPE
C_ALL = C_ROW + TAB

RSQRT_LINKS = 12
LN1_LINKS = 2 + RSQRT_LINKS
ROPE_LINKS = 3
HID_LINKS = 3
MID_LINKS = 1 + RSQRT_LINKS + 1 + 1 + RSQRT_LINKS
FIRST = 4
ROUTE_LINKS = 15


def hold(eng, sem, value, passed):
    eng.wait_ge(sem, value)
    eng.sem_inc(passed, 1)


class Chain:

    def __init__(self, eng, sem, done, links, passed=None):
        self.eng, self.sem, self.done, self.links, self.n, self.passed = eng, sem, done, links, 0, passed

    def __call__(self, ins, own=False):
        self.n += 1
        ins.then_inc(self.sem, 1)
        self.eng.wait_ge(self.sem, self.done * self.links + self.n)
        if own:
            self.eng.sem_inc(self.passed, 1)

    def end(self):
        assert self.n == self.links, (self.n, self.links)


def rsqrt(ch, out, var, work):
    dve = ch.eng
    v, y, t = work
    ch(dve.tensor_scalar(v, var, EPS, None, ALU.add))
    ch(dve.tensor_scalar(t.bitcast(U32), v.bitcast(U32), 1, None, ALU.logical_shift_right))
    ch(dve.tensor_scalar(y.bitcast(I32), t.bitcast(I32), -1.0, RSQRT_MAGIC, ALU.mult, ALU.add))
    for n in range(3):
        ch(dve.tensor_tensor(t, y, y, ALU.mult))
        ch(dve.scalar_tensor_tensor(out=t, in0=t, scalar=-0.5, in1=v, op0=ALU.mult, op1=ALU.mult))
        ch(dve.scalar_tensor_tensor(out=y if n < 2 else out, in0=t, scalar=1.5, in1=y,
                                    op0=ALU.add, op1=ALU.mult))


def build(nc, x_in, wqT, wkT, fc1_w, fc1_b, fc2_wT, fc2_b, low_rows, gate_w, gate_b, w1, b1T, w2, b2,
          cos_t, sin_t, ident_c, mask_c, tri_c, out):
    x_rows = x_in.rearrange("b l d -> (b l) d")
    out_rows = out.rearrange("b l d -> (b l) d")
    sorted_x = nc.dram_tensor("sorted_x", [NE * REGION, XW], F32).ap()
    pair_y = nc.dram_tensor("pair_y", [2 * NT, D], F32).ap()

    with ExitStack() as ctx:
        def sb(name, shape, dt, c=ctx):
            return c.enter_context(nc.sbuf_tensor(name, shape, dt))

        def sem(name, c=ctx):
            return c.enter_context(nc.semaphore(name))

        x_all = sb("x_all", [P, TT, D], F32)
        attn_shift = sb("attn_shift", [P, TT], F32)
        ident = sb("ident", [P, P], F32)
        b2_all = sb("b2_all", [P, NE, D], F32)
        b1_all = sb("b1_all", [P, NE, FC], F32)
        b1_now = [sb(f"b1_now{i}", [P, FC], F32) for i in range(2)]
        iota_e = sb("iota_e", [P, NE], F32)
        steer = sb("steer", [1, C_ALL], I32)
        w_stage = [sb(f"w_stage{i}", [P, 2, FC * D], F32) for i in range(2)]
        w_hi = [sb("w_hi0", [P, 2, FC * D], F32R), None]
        w_lo = [sb("w_lo0", [P, 2, FC * D], F32R), None]
        weights_in = [sem(f"weights_in{i}") for i in range(2)]
        w_hi_ready = [sem("w1_hi_ready"), sem("w2_hi_ready")]
        w_split = [sem("w1_split"), sem("w2_split")]
        b1_taken = sem("b1_taken")
        passed = sem("passed")

        def load_weights(sp, e, par):
            sp.dma_start(w_stage[par][:, 0, :].rearrange("p (k f) -> p k f", k=KC),
                         w1[bass.ds(e, 1), :, :].rearrange("e (k p) f -> p (e k) f", p=P)).then_inc(weights_in[par], 16)
            sp.dma_start(w_stage[par][:, 1, :].rearrange("p (c d) -> p c d", c=FC),
                         w2[bass.ds(e, 1), :, :].rearrange("e (c p) d -> p (e c) d", p=P)).then_inc(weights_in[par], 16)

        def low_part(eng, e, par, i):
            eng.wait_ge(w_hi_ready[i], e + 1)
            eng.tensor_tensor(w_lo[par][:, i, :], w_stage[par][:, i, :],
                              w_hi[par][:, i, :].bitcast(F32), ALU.subtract).then_inc(w_split[i], 1)

        def split_on_act(act, e, par, loads):
            act.wait_ge(weights_in[par], loads * 32)
            act.activation(w_hi[par][:, 0, :], w_stage[par][:, 0, :], ACT.Copy).then_inc(w_hi_ready[0], 1)
            act.activation(b1_now[par][:], b1_all[:, bass.ds(e, 1), :].rearrange("p e c -> p (e c)"),
                           ACT.Copy).then_inc(b1_taken, 1)

        def split_on_dve(dve, e, par, loads):
            dve.wait_ge(weights_in[par], loads * 32)
            dve.tensor_copy(w_hi[par][:, 1, :], w_stage[par][:, 1, :]).then_inc(w_hi_ready[1], 1)
            low_part(dve, e, par, 0)

        with ExitStack() as actx:
            def sa(name, shape, dt):
                return sb(name, shape, dt, actx)

            def pa(name, shape, dt):
                return actx.enter_context(nc.psum_tensor(name, shape, dt))

            def sm(name):
                return sem(name, actx)

            wqk = sa("wqk", [P, KC, 2, D], F32)
            wqk_hi = sa("wqk_hi", [P, KC, 2, D], F32R)
            wqk_lo = sa("wqk_lo", [P, KC, 2, D], F32R)
            cos_sb = sa("cos_sb", [P, L], BF16)
            sin_sb = sa("sin_sb", [P, L], BF16)
            identb = sa("identb", [P, P], BF16)
            mask = sa("mask", [P, P], BF16)
            tri = sa("tri", [P, P], BF16)
            ones = sa("ones", [P, P], BF16)
            fc1w = sa("fc1w", [P, INNER], F32)
            fc1b = sa("fc1b", [P, INNER], F32)
            fc2 = sa("fc2", [P, D], F32)
            fc2_hi = sa("fc2_hi", [P, D], F32R)
            fc2_parts = sa("fc2_parts", [P, D], F32R)
            lowrow = sa("lowrow", [P, 1], F32)
            gatew = sa("gatew", [P, KC, NE], F32)
            gateb = sa("gateb", [P, NE], F32)
            ids_i = sa("ids_i", [P, TT], I32)
            ids = sa("ids", [P, TT], F32)
            iota_i = sa("iota_i", [P, NE], I32)
            giota_i = sa("giota_i", [1, TAB], I32)
            giota = sa("giota", [1, TAB], F32)
            fill = sa("fill", [P, TM // P, XW], F32)

            stats = sa("stats", [P, TB, 6], F32)
            mv = sa("mv", [P, TB, 2], F32)
            rstd = sa("rstd", [P, TB], F32)
            shift = sa("shift", [P, TB], F32)
            nwork = sa("nwork", [P, 3, TB], F32)
            xn = sa("xn", [P, TB, D], F32)
            xT_hi = sa("xT_hi", [P, KC, L], F32R)
            xT_lo = sa("xT_lo", [P, KC, L], F32R)
            qk = sa("qk", [P, 2, KC, L], BF16)
            rope_a = sa("rope_a", [P, 2, L], BF16)
            rope_b = sa("rope_b", [P, 2, L], BF16)
            qkr = sa("qkr", [P, 2, KC, L], BF16)
            probs = sa("probs", [P, L], BF16)
            osum = sa("osum", [P, TB], F32)
            hid16 = sa("hid16", [P, TB, INNER], F32)
            hid = sa("hid", [P, TB, HID], F32)
            hidT = sa("hidT", [P, TB // 2, P], F32R)
            mstats = sa("mstats", [P, TB, 6], F32)
            mmv = sa("mmv", [P, TB, 2], F32)
            mrstd = sa("mrstd", [P, 2, TB], F32)
            mshift = sa("mshift", [P, TB], F32)
            mwork = sa("mwork", [P, 3, TB], F32)
            xrow = sa("xrow", [P, TB, XW], F32)
            x3T = sa("x3T", [P, KC, L], F32)
            logits = sa("logits", [P, TB, NE], F32)
            top8 = sa("top8", [P, TB, 8], F32)
            idx8 = sa("idx8", [P, TB, 8], U32)
            idxf = sa("idxf", [P, 2, TB], F32)
            onehot = sa("onehot", [P, 2, TB, NE], F32)
            chosen = sa("chosen", [P, TB, NE], BF16)
            scan_in = sa("scan_in", [P, NE, TB + 1], F32)
            scan_keep = sa("scan_keep", [P, NE, TB + 1], F32)
            carry = sa("carry", [P, NE, TB + 1], F32)
            pos = sa("pos", [P, TB, NE], F32)
            slot_w = sa("slot_w", [P, 2, TB, NE], F32)
            slot = sa("slot", [P, 2 * TB], F32)
            slot_i = sa("slot_i", [P, 2 * TB], I32)
            gdiff = sa("gdiff", [P, TB], F32)
            gexp = sa("gexp", [P, TB], F32)
            gden = sa("gden", [P, TB], F32)
            cnt = sa("cnt", [1, 6, NE + 1], F32)
            cnt_i = sa("cnt_i", [1, 2, NE], I32)
            gm = x3T[0:1].rearrange("p k n -> p (k n)")[:, 0:3 * TAB * NE].rearrange("p (i n) -> p i n", i=3)

            pT = pa("pT", [P, 2, 512], F32)
            pP = pa("pP", [P, 2, 512], F32)
            pS = pa("pS", [P, 4, 512], F32)
            pA = pS[:, :, :].rearrange("p b (u d) -> p (b u) d", d=D)
            pLog = pP[:, 0, 0:TB * NE]
            pRank = pP[:, 1, 0:TB * NE]
            pTot = pP[:, 1, TB * NE:2 * TB * NE]

            x_first = sm("x_first")
            x_rest = sm("x_rest")
            wqk_in = sm("wqk_in")
            consts_in = sm("consts_in")
            b2_in = sm("b2_in")
            tables_in = sm("tables_in")
            pool_set = sm("pool_set")
            set_up = sm("set_up")
            ln1_link = sm("ln1_link")
            xn_stats = sm("xn_stats")
            xn_ready = sm("xn_ready")
            xn_turned = sm("xn_turned")
            xT_hi_ready = sm("xT_hi_ready")
            xT_ready = sm("xT_ready")
            projected = sm("projected")
            qk_ready = sm("qk_ready")
            rope_link = sm("rope_link")
            roped = sm("roped")
            scored = sm("scored")
            summed = sm("summed")
            mid_link = sm("mid_link")
            hid_link = sm("hid_link")
            attn_measured = sm("attn_measured")
            hid_ready = sm("hid_ready")
            hid_turned = sm("hid_turned")
            hidT_ready = sm("hidT_ready")
            mlp_done = sm("mlp_done")
            attn_added = sm("attn_added")
            x3_stats = sm("x3_stats")
            x3_ready = sm("x3_ready")
            x3_turned = sm("x3_turned")
            x3T_ready = sm("x3T_ready")
            logits_done = sm("logits_done")
            route_link = sm("route_link")
            gdiff_ready = sm("gdiff_ready")
            gexp_ready = sm("gexp_ready")
            chosen_ready = sm("chosen_ready")
            ranked = sm("ranked")
            ranks_read = sm("ranks_read")
            rows_ready = sm("rows_ready")
            rows_sent = sm("rows_sent")
            rows_left = sm("rows_left")
            steer_link = sm("steer_link")
            steer_ready = sm("steer_ready")
            ends_filled = sm("ends_filled")

            CONSTS = 7 + 12
            with nc.Block() as block:

                @block.sync
                def _(sp):
                    sp.dma_start(x_all[:, 0:TB, :], x_rows[0:L, :].rearrange("(t p) d -> p t d", p=P)).then_inc(x_first, 16)
                    for i, w in enumerate((wqT, wkT)):
                        sp.dma_start(wqk[:, :, i, :], w.rearrange("(k p) d -> p k d", p=P)).then_inc(wqk_in, 16)
                    for dst, src in ((ident[:], ident_c),
                                     (fc1w[:], fc1_w.rearrange("i o -> o i").to_broadcast([P, INNER])),
                                     (fc1b[:], fc1_b.rearrange("(o i) -> o i", o=1).to_broadcast([P, INNER])),
                                     (gatew[:], gate_w.rearrange("(k p) e -> p k e", p=P)),
                                     (gateb[:], gate_b.rearrange("(o e) -> o e", o=1).to_broadcast([P, NE])),
                                     (lowrow[:], low_rows),
                                     (b1_all[:], b1T)):
                        sp.dma_start(dst, src).then_inc(consts_in, 16)
                    for j in range(2):
                        for i in range(3):
                            at = HID * j + HK * i
                            sp.dma_start(fc2[at:at + INNER, :], fc2_wT).then_inc(consts_in, 16)
                            sp.dma_start(fc2[at + INNER:at + HK, :],
                                         fc2_b.rearrange("(o d) -> o d", o=1)).then_inc(consts_in, 16)
                    for b in range(1, B):
                        sp.dma_start(x_all[:, b * TB:(b + 1) * TB, :],
                                     x_rows[b * L:(b + 1) * L, :].rearrange("(t p) d -> p t d", p=P)).then_inc(x_rest, 16)
                    sp.dma_start(b2_all[:].rearrange("p e d -> p (e d)"),
                                 b2.rearrange("e d -> (e d)").rearrange("(o n) -> o n", o=1).to_broadcast([P, NE * D])
                                 ).then_inc(b2_in, 16)
                    for e in range(2):
                        load_weights(sp, e, e)
                    sp.wait_ge(pool_set, 8)
                    sp.wait_ge(steer_ready, 1)
                    for e in range(NE):
                        end = sp.value_load(steer[0:1, C_END + e:C_END + e + 1], min_val=e * REGION,
                                            max_val=e * REGION + NT)
                        sp.dma_start(sorted_x[bass.ds(end, TM), :].rearrange("(a p) c -> p a c", p=P),
                                     fill[:]).then_inc(ends_filled, 16)
                    sp.wait_ge(ends_filled, 16 * NE)
                    sp.wait_ge(b2_in, 16)

                @block.gpsimd
                def _(pool):
                    pool.sem_inc(rows_left, ONE)
                    for dst, src in ((cos_sb, cos_t), (sin_sb, sin_t), (mask, mask_c), (tri, tri_c)):
                        pool.dma_start(dst[:], src).then_inc(tables_in, 16)
                    pool.memset(ones[:], 1.0).then_inc(pool_set, 1)
                    pool.memset(hid[:], 0.0).then_inc(pool_set, 1)
                    pool.memset(fill[:], 0.0).then_inc(pool_set, 1)
                    pool.iota(ids_i[:], pattern=[[P, TT]], base=0, channel_multiplier=1).then_inc(pool_set, 1)
                    pool.iota(iota_i[:], pattern=[[1, NE]], base=0, channel_multiplier=0).then_inc(pool_set, 1)
                    pool.iota(giota_i[:], pattern=[[1, TAB]], base=0, channel_multiplier=0).then_inc(pool_set, 1)
                    pool.wait_ge(pool_set, 6)
                    pool.memset(fill[:, :, D:D + 1], NO_TOKEN).then_inc(pool_set, 1)
                    pool.memset(fill[:, :, D + 1:D + 2], -1.0).then_inc(pool_set, 1)
                    low_part(pool, 0, 0, 1)

                    with pool.Fori(0, B) as b:
                        hold(pool, rows_ready, b + 1, passed)
                        for i in range(2 * TB):
                            pool.indirect_dma_start(
                                out=sorted_x, out_offset=bass.IndirectOffsetOnAxis(ap=slot_i[:, i:i + 1], axis=0),
                                in_=xrow[:, i % TB, :], in_offset=None).then_inc(rows_sent, 16)
                        hold(pool, rows_sent, (b + 1) * (2 * TB * 16), rows_left)

                @block.scalar
                def _(act):
                    act.sem_inc(gexp_ready, ONE)
                    def norm_x(b):
                        act.wait_ge(xn_stats, b + 1)
                        act.wait_ge(xn_turned, b * 4)
                        for t in range(TB):
                            act.activation(xn[:, t, :], x_all[:, b * TB + t, :], ACT.Identity, bias=shift[:, t:t + 1],
                                           scale=rstd[:, t:t + 1]).then_inc(xn_ready, 1)

                    def turn_hi(b):
                        act.wait_ge(projected, b * 8)
                        for n in range(2 * KC):
                            h, k = n // KC, n % KC
                            act.wait_ge(xn_turned, b * 4 + n + 1)
                            act.activation(xT_hi[:, k, h * 512:(h + 1) * 512], pT[:, n % 2, :],
                                           ACT.Copy).then_inc(xT_hi_ready, 1)

                    def take_qk(b, roped_before):
                        act.wait_ge(roped, roped_before)
                        for n in range(8):
                            h, i, m = n // 4, (n // 2) % 2, n % 2
                            act.wait_ge(projected, b * 8 + n + 1)
                            act.activation(qk[:, i, m, h * 512:(h + 1) * 512], pP[:, n % 2, :],
                                           ACT.Copy).then_inc(qk_ready, 1)

                    def sum_exps(b, tiles):
                        act.wait_ge(hid_ready, b + ONE)
                        for t in tiles:
                            act.wait_ge(scored, b * TB + t + 1)
                            act.wait_ge(summed, b * TB + t)
                            n = (t + 1) * P
                            act.activation(probs[:, 0:n],
                                           pS[:, 2 * (t % 2):2 * (t % 2) + 2, :].rearrange("p b n -> p (b n)")[:, 0:n],
                                           ACT.Exp, scale=1.0 / D ** 0.5,
                                           accum_out=osum[:, t:t + 1]).then_inc(summed, 1)

                    def take_hid(c):
                        act.wait_ge(hid_turned, c + 1 + ONE)
                        act.activation(hidT[:].rearrange("p g n -> p (g n)"), pT[:, 0, :],
                                       ACT.Copy).then_inc(hidT_ready, 1)

                    def norm_x3(c):
                        act.wait_ge(x3_stats, c + 1)
                        act.wait_ge(rows_left, c + ONE)
                        for t in range(TB):
                            act.activation(xrow[:, t, 0:D], x_all[:, c * TB + t, :], ACT.Identity,
                                           bias=mshift[:, t:t + 1],
                                           scale=mrstd[:, 1, t:t + 1]).then_inc(x3_ready, 1)
                        for n in range(2 * KC):
                            h, k = n // KC, n % KC
                            act.wait_ge(x3_turned, c * 4 + n + 1)
                            act.activation(x3T[:, k, h * 512:(h + 1) * 512], pT[:, n % 2, :],
                                           ACT.Copy).then_inc(x3T_ready, 1)

                    def weigh(c):
                        act.wait_ge(gdiff_ready, c + 1)
                        act.activation(gexp[:], gdiff[:], ACT.Exp).then_inc(gexp_ready, 1)

                    act.wait_ge(consts_in, 16 * CONSTS)
                    norm_x(0)
                    turn_hi(0)
                    take_qk(0, 0)
                    sum_exps(0, range(TB))
                    split_on_act(act, 0, 0, 1)
                    with act.Fori(0, B - 1) as j:
                        take_hid(j)
                        norm_x(j + 1)
                        turn_hi(j + 1)
                        take_qk(j + 1, j + 1)
                        norm_x3(j)
                        sum_exps(j + 1, range(FIRST))
                        weigh(j)
                        sum_exps(j + 1, range(FIRST, TB))
                    take_hid(B - 1)
                    norm_x3(B - 1)
                    weigh(B - 1)

                @block.tensor
                def _(pe):
                    pe.sem_inc(hid_turned, ONE)
                    def turn_x(b):
                        for n in range(2 * KC):
                            h, k = n // KC, n % KC
                            if n >= 2:
                                pe.wait_ge(xT_ready, b * 4 + n - 1)
                            for u in range(4):
                                t = 4 * h + u
                                if k == 0:
                                    pe.wait_ge(xn_ready, b * TB + t + 1)
                                mm = pe.transpose(pT[:, n % 2, u * P:(u + 1) * P], xn[:, t, k * P:(k + 1) * P], ident[:])
                            mm.then_inc(xn_turned, 1)

                    def project(b, routed):
                        pe.wait_ge(ranks_read, routed + ONE)
                        for n in range(8):
                            h, i, m = n // 4, (n // 2) % 2, n % 2
                            pe.wait_ge(xT_ready, b * 4 + 2 * (h + 1))
                            if n >= 2:
                                pe.wait_ge(qk_ready, b * 8 + n - 1)
                            tok = slice(h * 512, (h + 1) * 512)
                            mo = slice(m * P, (m + 1) * P)
                            for k in range(KC):
                                for w, x in ((wqk_lo, xT_hi), (wqk_hi, xT_hi), (wqk_hi, xT_lo)):
                                    mm = pe.matmul(pP[:, n % 2, :], w[:, k, i, mo], x[:, k, tok],
                                                   start=(k == 0 and w is wqk_lo), stop=(k == KC - 1 and x is xT_lo))
                            mm.then_inc(projected, 1)

                    def score(b, tiles):
                        pe.wait_ge(roped, b + 1)
                        pe.wait_ge(attn_added, b * TB)
                        for t in tiles:
                            if t >= 2:
                                pe.wait_ge(summed, b * TB + t - 1)
                            keys = (t + 1) * P
                            for a in range(0, keys, 512):
                                n = min(512, keys - a)
                                bank = pS[:, 2 * (t % 2) + a // 512, :]
                                last = a + n == keys
                                for m in range(KC):
                                    mm = pe.matmul(bank[:, 0:n], qkr[:, 0, m, t * P:(t + 1) * P],
                                                   qkr[:, 1, m, a:a + n], start=(m == 0), stop=(m == KC - 1 and not last))
                                if last:
                                    mm = pe.matmul(bank[:, n - P:n], identb[:], mask[:], start=False, stop=True)
                            mm.then_inc(scored, 1)

                    def attention_mlp(c):
                        pe.wait_ge(hid_ready, c + 1 + ONE)
                        for g in range(TB // 2):
                            mm = pe.transpose(pT[:, 0, g * P:(g + 1) * P],
                                              hid[:, 2 * g:2 * g + 2, :].rearrange("p t h -> p (t h)"), ident[:])
                        mm.then_inc(hid_turned, 1)
                        pe.wait_ge(hidT_ready, c + 1)
                        pe.wait_ge(summed, (c + 1) * TB)
                        for g in range(TB // 2):
                            for j in range(2):
                                rows = slice(HID * j, HID * j + 3 * HK)
                                mm = pe.matmul(pA[:, 4 * j + g, :], hidT[rows, g, :], fc2_parts[rows, :],
                                               start=True, stop=True)
                            if g % 2 == 1:
                                mm.then_inc(mlp_done, 1)

                    def gate(c, fronts):
                        for n in range(2 * KC):
                            h, k = n // KC, n % KC
                            if n >= 2:
                                pe.wait_ge(x3T_ready, c * 4 + n - 1)
                            for u in range(4):
                                t = 4 * h + u
                                if k == 0:
                                    pe.wait_ge(x3_ready, c * TB + t + 1)
                                mm = pe.transpose(pT[:, n % 2, u * P:(u + 1) * P], xrow[:, t, k * P:(k + 1) * P], ident[:])
                            mm.then_inc(x3_turned, 1)
                        pe.wait_ge(x3T_ready, (c + 1) * 4)
                        pe.wait_ge(qk_ready, fronts * 8)
                        for t in range(TB):
                            for k in range(KC):
                                mm = pe.matmul(pLog[:, t * NE:(t + 1) * NE], x3T[:, k, t * P:(t + 1) * P],
                                               gatew[:, k, :], start=(k == 0), stop=(k == KC - 1))
                        mm.then_inc(logits_done, 1)

                    def rank(c):
                        pe.wait_ge(chosen_ready, c + 1)
                        ch = chosen[:].rearrange("p t e -> p (t e)")
                        pe.matmul(pRank, tri[:], ch, start=True, stop=True)
                        pe.matmul(pTot, ones[:], ch, start=True, stop=True).then_inc(ranked, 1)

                    pe.wait_ge(tables_in, 64)
                    pe.wait_ge(consts_in, 16 * CONSTS)
                    pe.wait_ge(set_up, 4)
                    turn_x(0)
                    project(0, 0)
                    score(0, range(TB))
                    pe.wait_ge(set_up, 8)
                    with pe.Fori(0, B - 1) as j:
                        attention_mlp(j)
                        turn_x(j + 1)
                        project(j + 1, j)
                        gate(j, j + 2)
                        score(j + 1, range(FIRST))
                        rank(j)
                        score(j + 1, range(FIRST, TB))
                    attention_mlp(B - 1)
                    gate(B - 1, B)
                    rank(B - 1)

                @block.vector
                def _(dve):
                    dve.sem_inc(hid_ready, ONE)
                    dve.sem_inc(ranks_read, ONE)
                    def stats_x(b):
                        ch = Chain(dve, ln1_link, b, LN1_LINKS, passed)
                        for t in range(TB):
                            s = dve.bn_stats(stats[:, t, :], x_all[:, b * TB + t, :])
                        ch(s, own=True)
                        for t in range(TB):
                            s = dve.bn_aggr(mv[:, t, :], stats[:, t, :])
                        ch(s)
                        dve.wait_ge(xn_ready, b * TB)
                        rsqrt(ch, rstd[:], mv[:, :, 1], [nwork[:, i, :] for i in range(3)])
                        dve.scalar_tensor_tensor(out=shift[:], in0=mv[:, :, 0], scalar=-1.0, in1=rstd[:],
                                                 op0=ALU.mult, op1=ALU.mult).then_inc(xn_stats, 1)
                        ch.end()

                    def turn_lo(b):
                        for n in range(2 * KC):
                            h, k = n // KC, n % KC
                            dve.wait_ge(xT_hi_ready, b * 4 + n + 1)
                            tok = slice(h * 512, (h + 1) * 512)
                            dve.tensor_tensor(xT_lo[:, k, tok], pT[:, n % 2, :], xT_hi[:, k, tok].bitcast(F32),
                                              ALU.subtract).then_inc(xT_ready, 1)

                    def rope(b):
                        dve.wait_ge(qk_ready, (b + 1) * 8)
                        dve.wait_ge(scored, b * TB)
                        co = cos_sb[:].rearrange("p (o n) -> p o n", o=1).to_broadcast([P, 2, L])
                        si = sin_sb[:].rearrange("p (o n) -> p o n", o=1).to_broadcast([P, 2, L])
                        ch = Chain(dve, rope_link, b, ROPE_LINKS)
                        for m, op in ((0, ALU.subtract), (1, ALU.add)):
                            dve.tensor_tensor(rope_a[:], qk[:, :, m, :], co, ALU.mult)
                            ch(dve.tensor_tensor(rope_b[:], qk[:, :, 1 - m, :], si, ALU.mult))
                            last = dve.tensor_tensor(qkr[:, :, m, :], rope_a[:], rope_b[:], op)
                            if m == 0:
                                ch(last)
                        ch.end()
                        last.then_inc(roped, 1)

                    def hidden(c):
                        dve.wait_ge(summed, (c + 1) * TB)
                        dve.wait_ge(hid_turned, c + ONE)
                        ch = Chain(dve, hid_link, c, HID_LINKS)
                        ch(dve.tensor_tensor(hid16[:], osum[:].rearrange("p (t o) -> p t o", o=1).to_broadcast([P, TB, INNER]),
                                             fc1w[:].rearrange("p (o i) -> p o i", o=1).to_broadcast([P, TB, INNER]),
                                             ALU.mult))
                        ch(dve.tensor_tensor(hid16[:], hid16[:],
                                             fc1b[:].rearrange("p (o i) -> p o i", o=1).to_broadcast([P, TB, INNER]),
                                             ALU.add))
                        hi, lo, hi2 = (hid[:, :, HK * i:HK * i + INNER].bitcast(F32R) for i in range(3))
                        dve.tensor_scalar(hi2, hid16[:], 0.0, None, ALU.max)
                        ch(dve.tensor_scalar(hi, hid16[:], 0.0, None, ALU.max))
                        dve.scalar_tensor_tensor(out=lo, in0=hid16[:], scalar=0.0, in1=hi.bitcast(F32),
                                                 op0=ALU.max, op1=ALU.subtract).then_inc(hid_ready, 1)
                        ch.end()

                    def stats_attn(c):
                        for g in range(TB // 2):
                            if g % 2 == 0:
                                dve.wait_ge(mlp_done, c * (TB // 4) + g // 2 + 1)
                            for j in range(2):
                                s = dve.bn_stats(mstats[:, 2 * g + j, :], pA[:, 4 * j + g, :])
                        s.then_inc(attn_measured, 1)

                    def mid(c):
                        def scale(ch, i):
                            for t in range(TB):
                                s = dve.bn_aggr(mmv[:, t, :], mstats[:, t, :])
                            ch(s)
                            rsqrt(ch, mrstd[:, i, :], mmv[:, :, 1], [mwork[:, i, :] for i in range(3)])

                        hold(dve, attn_measured, c + 1, passed)
                        ch = Chain(dve, mid_link, c, MID_LINKS, passed)
                        scale(ch, 0)
                        dve.scalar_tensor_tensor(out=attn_shift[:, bass.ds(c * TB, TB)], in0=mmv[:, :, 0], scalar=-1.0,
                                                 in1=mrstd[:, 0, :], op0=ALU.mult, op1=ALU.mult)
                        for t in range(TB):
                            xt = x_all[:, c * TB + t, :]
                            s = dve.scalar_tensor_tensor(out=xt, in0=pA[:, 4 * (t % 2) + t // 2, :],
                                                         scalar=mrstd[:, 0, t:t + 1], in1=xt,
                                                         op0=ALU.mult, op1=ALU.add).then_inc(attn_added, 1)
                        hold(dve, attn_added, (c + 1) * TB, passed)
                        for t in range(TB):
                            s = dve.bn_stats(mstats[:, t, :], x_all[:, c * TB + t, :])
                        ch(s, own=True)
                        scale(ch, 1)
                        dve.wait_ge(x3_ready, c * TB)
                        dve.scalar_tensor_tensor(out=mshift[:], in0=mmv[:, :, 0], scalar=-1.0, in1=mrstd[:, 1, :],
                                                 op0=ALU.mult, op1=ALU.mult).then_inc(x3_stats, 1)
                        ch.end()

                    def route(c):
                        ch = Chain(dve, route_link, c, ROUTE_LINKS, passed)
                        dve.wait_ge(logits_done, c + 1)
                        ch(dve.tensor_tensor(logits[:], pLog.rearrange("p (t e) -> p t e", e=NE),
                                             gateb[:].rearrange("p (o e) -> p o e", o=1).to_broadcast([P, TB, NE]), ALU.add),
                           own=True)
                        for t in range(TB):
                            s = dve.max(top8[:, t, :], logits[:, t, :])
                        ch(s, own=True)
                        for t in range(TB):
                            s = dve.max_index(idx8[:, t, :], top8[:, t, :], logits[:, t, :])
                        ch(s)
                        dve.wait_ge(gexp_ready, c + ONE)
                        dve.tensor_tensor(gdiff[:], top8[:, :, 1], top8[:, :, 0], ALU.subtract).then_inc(gdiff_ready, 1)
                        ch(dve.tensor_copy(idxf[:], idx8[:, :, 0:2].rearrange("p t k -> p k t")))
                        io = iota_e[:].rearrange("p (o e) -> p o e", o=1).to_broadcast([P, TB, NE])
                        for k in range(2):
                            s = dve.tensor_tensor(onehot[:, k], io,
                                                  idxf[:, k, :].rearrange("p (t o) -> p t o", o=1).to_broadcast([P, TB, NE]),
                                                  ALU.is_equal)
                        ch(s)
                        dve.tensor_tensor(chosen[:], onehot[:, 0], onehot[:, 1], ALU.add).then_inc(chosen_ready, 1)
                        dve.wait_ge(ranked, c + 1)
                        ch(dve.tensor_copy(scan_in[:, :, 1:TB + 1], pTot.rearrange("p (t e) -> p e t", e=NE)))
                        ch(dve.tensor_tensor_scan(carry[:].rearrange("p e t -> p (e t)"),
                                                  scan_keep[:].rearrange("p e t -> p (e t)"),
                                                  scan_in[:].rearrange("p e t -> p (e t)"), 0.0, ALU.mult, ALU.add))
                        dve.tensor_tensor(pos[:], pRank.rearrange("p (t e) -> p t e", e=NE),
                                          carry[:, :, 0:TB].rearrange("p e t -> p t e"), ALU.add).then_inc(ranks_read, 1)
                        ch(dve.tensor_copy(scan_in[:, :, 0:1], carry[:, :, TB:TB + 1]))
                        dve.wait_ge(ranks_read, c + 1 + ONE)
                        for k in range(2):
                            s = dve.tensor_tensor(slot_w[:, k], onehot[:, k], pos[:], ALU.mult)
                        ch(s)
                        ch(dve.tensor_reduce(slot[:], slot_w[:].rearrange("p k t e -> p (k t) e"), AX_X, ALU.add))
                        dve.wait_ge(rows_left, c + ONE)
                        ch(dve.tensor_copy(slot_i[:], slot[:]))
                        dve.wait_ge(x3_ready, (c + 1) * TB)
                        ch(dve.tensor_copy(xrow[:, :, D], ids[:, bass.ds(c * TB, TB)]))
                        ch(dve.tensor_copy(xrow[:, :, D + 1], idxf[:, 0, :]))
                        dve.wait_ge(gexp_ready, c + 1 + ONE)
                        ch(dve.tensor_scalar(gden[:], gexp[:], 1.0, None, ALU.add))
                        ch(dve.reciprocal(xrow[:, :, D + 2], gden[:]))
                        dve.tensor_tensor(xrow[:, :, D + 3], gexp[:], xrow[:, :, D + 2],
                                          ALU.mult).then_inc(rows_ready, 1)
                        ch.end()

                    def steer_table():
                        n = [0]

                        def ch(ins):
                            n[0] += 1
                            ins.then_inc(steer_link, 1)
                            dve.wait_ge(steer_link, n[0])

                        end, count, tiles, incl, base, keep = (cnt[:, i, 0:NE] for i in range(6))
                        ch(dve.tensor_copy(end, carry[0:1, :, TB]))
                        ch(dve.scalar_tensor_tensor(out=count, in0=iota_e[0:1, :], scalar=-float(REGION), in1=end,
                                                    op0=ALU.mult, op1=ALU.add))
                        ch(dve.tensor_scalar(cnt_i[:, 0, :], count, float(TM - 1), None, ALU.add))
                        ch(dve.tensor_scalar(cnt_i[:, 1, :], cnt_i[:, 0, :], int(np.log2(TM)), None,
                                             ALU.arith_shift_right))
                        ch(dve.tensor_copy(tiles, cnt_i[:, 1, :]))
                        ch(dve.memset(keep, 1.0))
                        ch(dve.tensor_tensor_scan(incl, keep, tiles, 0.0, ALU.mult, ALU.add))
                        ch(dve.tensor_tensor(base, incl, tiles, ALU.subtract))
                        for at, v in ((C_END, end), (C_TILES, tiles), (C_BASE, base)):
                            ch(dve.tensor_copy(steer[:, at:at + NE], v))
                        G = TAB
                        a, w, r = (gm[:, i, :].rearrange("o (g e) -> o g e", e=NE) for i in range(3))
                        gi = giota[:].rearrange("o (g u) -> o g u", u=1).to_broadcast([1, G, NE])

                        def per_e(v):
                            return v.rearrange("o (u e) -> o u e", u=1).to_broadcast([1, G, NE])

                        ch(dve.tensor_tensor(a, gi, per_e(base), ALU.is_ge))
                        ch(dve.tensor_tensor(w, gi, per_e(incl), ALU.is_lt))
                        ch(dve.tensor_tensor(a, a, w, ALU.mult))
                        ch(dve.tensor_tensor(w, gi, per_e(base), ALU.subtract))
                        ch(dve.tensor_scalar(w, w, float(TM), None, ALU.mult))
                        ch(dve.scalar_tensor_tensor(out=r, in0=per_e(iota_e[0:1, :]), scalar=float(REGION), in1=w,
                                                    op0=ALU.mult, op1=ALU.add))
                        ch(dve.tensor_tensor(r, r, a, ALU.mult))
                        ch(dve.tensor_reduce(gm[:, 1, 0:G], r, AX_X, ALU.add))
                        ch(dve.tensor_reduce(gm[:, 2, 0:G], a, AX_X, ALU.add))
                        ch(dve.tensor_scalar(gm[:, 2, 0:G], gm[:, 2, 0:G], -1.0, 1.0, ALU.mult, ALU.add))
                        ch(dve.scalar_tensor_tensor(out=gm[:, 1, 0:G], in0=gm[:, 2, 0:G], scalar=end[:, 0:1],
                                                    in1=gm[:, 1, 0:G], op0=ALU.mult, op1=ALU.add))
                        dve.tensor_copy(steer[:, C_ROW:C_ROW + G], gm[:, 1, 0:G]).then_inc(steer_ready, 1)

                    dve.wait_ge(wqk_in, 32)
                    dve.tensor_copy(wqk_hi[:], wqk[:]).then_inc(set_up, 1)
                    dve.wait_ge(set_up, 1)
                    dve.tensor_tensor(wqk_lo[:], wqk[:], wqk_hi[:].bitcast(F32), ALU.subtract).then_inc(set_up, 1)
                    dve.wait_ge(pool_set, 8)
                    for i in range(0, 3, 2):
                        at = HK * i + INNER
                        dve.tensor_scalar(hid[:, :, at], hid[:, :, HID - 1], 1.0, None, ALU.add)
                    dve.tensor_copy(ids[:], ids_i[:])
                    dve.tensor_copy(giota[:], giota_i[:])
                    dve.memset(scan_keep[:], 1.0)
                    dve.tensor_copy(iota_e[:], iota_i[:]).then_inc(set_up, 1)
                    dve.wait_ge(set_up, 3)
                    dve.tensor_scalar(scan_in[:, :, 0], iota_e[:], float(REGION), None, ALU.mult)
                    dve.memset(scan_keep[:, :, 0:1], 0.0)
                    dve.wait_ge(tables_in, 64)
                    dve.wait_ge(consts_in, 16 * CONSTS)
                    dve.tensor_copy(identb[:], ident[:]).then_inc(set_up, 1)
                    dve.wait_ge(set_up, 4)
                    dve.wait_ge(x_first, 16)
                    stats_x(0)
                    for j in range(2):
                        rows = slice(HID * j, HID * j + 3 * HK)
                        dve.tensor_copy(fc2_hi[rows, :], fc2[rows, :]).then_inc(set_up, 1)
                    dve.wait_ge(set_up, 6)
                    for j in range(2):
                        rows = slice(HID * j, HID * j + 3 * HK)
                        dve.scalar_tensor_tensor(out=fc2_parts[rows, :], in0=fc2_hi[rows, :].bitcast(F32),
                                                 scalar=lowrow[rows, 0:1], in1=fc2[rows, :],
                                                 op0=ALU.mult, op1=ALU.add).then_inc(set_up, 1)
                    turn_lo(0)
                    rope(0)
                    dve.wait_ge(x_rest, 16 * (B - 1))
                    stats_x(1)
                    split_on_dve(dve, 0, 0, 1)

                    def batch(j, more):
                        hidden(j)
                        stats_attn(j)
                        turn_lo(j + 1)
                        mid(j)
                        rope(j + 1)
                        if more:
                            stats_x(j + 2)
                        route(j)

                    with dve.Fori(0, B - 2) as j:
                        batch(j, True)
                    batch(B - 2, False)
                    hidden(B - 1)
                    stats_attn(B - 1)
                    mid(B - 1)
                    route(B - 1)
                    steer_table()

        with ExitStack() as ectx:
            def se(name, shape, dt):
                return sb(name, shape, dt, ectx)

            def pe_sum(name, shape, dt):
                return ectx.enter_context(nc.psum_tensor(name, shape, dt))

            def sm(name):
                return sem(name, ectx)

            w_hi[1] = se("w_hi1", [P, 2, FC * D], F32R)
            w_lo[1] = se("w_lo1", [P, 2, FC * D], F32R)
            xt = se("xt", [P, TM // P, XW], F32)
            xeT_hi = se("xeT_hi", [P, KC, TM], F32R)
            xeT_lo = se("xeT_lo", [P, KC, TM], F32R)
            h = se("h", [P, FC, TM], F32)
            h_hi = se("h_hi", [P, FC, TM], F32R)
            h_lo = se("h_lo", [P, FC, TM], F32R)
            tag = se("tag", [P, TM // P, 4], F32)
            other = se("other", [P, TM // P], F32)
            same = se("same", [P, TM // P], F32)
            wa = se("wa", [P, TM // P], F32)
            wb = se("wb", [P, TM // P], F32)
            weight = se("weight", [P, TM // P], F32)
            dest = se("dest", [P, TM // P], I32)
            y = se("y", [P, TM // P, D], F32)
            pL = pe_sum("pL", [P, 4, 512], F32)
            pX = pe_sum("pX", [P, KC, TM], F32)
            pY = pe_sum("pY", [P, 2, 512], F32)

            tile_in = sm("tile_in")
            tile_turned = sm("tile_turned")
            tag_saved = sm("tag_saved")
            xeT_hi_ready = sm("xeT_hi_ready")
            xeT_ready = sm("xeT_ready")
            l1_done = sm("l1_done")
            h_ready = sm("h_ready")
            h_hi_ready = sm("h_hi_ready")
            h_split = sm("h_split")
            l2_done = sm("l2_done")
            tag_link = sm("tag_link")
            y_added = sm("y_added")
            y_ready = sm("y_ready")
            y_sent = sm("y_sent")
            y_left = sm("y_left")
            TAG_LINKS = 5

            def is_last(e):
                return type(e) is int and e == NE - 1

            def over_tiles(eng, start, tile):
                def expert(pair, par):
                    e = pair * 2 + par
                    n = eng.value_load(steer[0:1, bass.ds(C_TILES + e, 1)], min_val=0, max_val=TPE)
                    base = eng.value_load(steer[0:1, bass.ds(C_BASE + e, 1)], min_val=0, max_val=MAXG)
                    if start:
                        start(e, pair, par, base)

                    def bits(k):
                        with eng.If(n >= 1 << k):
                            with eng.If((n & (1 << k)) > 0):
                                first = base if k == 0 else base + (n & ((1 << k) - 1))
                                if k < 2:
                                    for v in range(1 << k):
                                        tile(e, par, first + v)
                                else:
                                    with eng.Fori(0, 1 << k - 1) as v:
                                        for i in range(2):
                                            tile(e, par, first + 2 * v + i)
                            if 2 << k <= TPE:
                                bits(k + 1)

                    bits(0)

                with eng.Fori(0, NE // 2 - 1) as pair:
                    for par in range(2):
                        expert(pair, par)
                for par in range(2):
                    expert(NE // 2 - 1, par)

            with nc.Block() as block:

                @block.sync
                def _(sp):
                    def load_tile(g):
                        row = sp.value_load(steer[0:1, bass.ds(C_ROW + g, 1)], min_val=0, max_val=NE * REGION - TM)
                        sp.dma_start(xt[:], sorted_x[bass.ds(row, TM), :].rearrange("(a p) c -> p a c", p=P)
                                     ).then_inc(tile_in, 16)

                    def start(e, pair, par, base):
                        if type(e) is not int:
                            for i in range(2):
                                sp.wait_ge(w_split[i], e + 1)
                            load_weights(sp, e + 2, par)

                    def tile(e, par, g):
                        sp.wait_ge(tile_turned, g + 1)
                        sp.wait_ge(tag_saved, g + 1)
                        load_tile(g + 1)

                    load_tile(0)
                    over_tiles(sp, start, tile)

                @block.gpsimd
                def _(pool):
                    pool.sem_inc(y_left, ONE)
                    def start(e, pair, par, base):
                        if not is_last(e):
                            pool.wait_ge(l2_done, 2 * base + ONE)
                            low_part(pool, e + 1, 1 - par, 1)

                    def tile(e, par, g):
                        for i in range(TM // P):
                            hold(pool, y_ready, 2 * g + i + 1, passed)
                            pool.indirect_dma_start(
                                out=pair_y, out_offset=bass.IndirectOffsetOnAxis(ap=dest[:, i:i + 1], axis=0),
                                in_=y[:, i, :], in_offset=None, bounds_check=2 * NT - 1,
                                oob_is_err=False).then_inc(y_sent, 16)
                        hold(pool, y_sent, (g + 1) * 32, y_left)

                    over_tiles(pool, start, tile)

                @block.scalar
                def _(act):
                    def turn_hi(g):
                        act.wait_ge(tile_turned, g + 1)
                        act.activation(xeT_hi[:], pX[:], ACT.Copy).then_inc(xeT_hi_ready, 1)

                    def start(e, pair, par, base):
                        if not is_last(e):
                            act.wait_ge(l2_done, 2 * base + ONE)
                            split_on_act(act, e + 1, 1 - par, pair + par + 1)

                    def tile(e, par, g):
                        act.wait_ge(b1_taken, e + 1)
                        act.wait_ge(h_split, 4 * g + ONE)
                        for bk in range(4):
                            act.wait_ge(l1_done, 4 * g + bk + 1)
                            for i in range(2):
                                c = 2 * bk + i
                                a = act.activation(h[:, c, :], pL[:, bk, i * TM:(i + 1) * TM], ACT.Gelu,
                                                   bias=b1_now[par][:, c:c + 1])
                            a.then_inc(h_ready, 1)
                        turn_hi(g + 1)

                    turn_hi(0)
                    over_tiles(act, start, tile)

                @block.tensor
                def _(pe):
                    pe.sem_inc(l2_done, ONE)
                    def turn(g):
                        pe.wait_ge(tile_in, 16 * (g + 1))
                        for k in range(KC):
                            for i in range(TM // P):
                                mm = pe.transpose(pX[:, k, i * P:(i + 1) * P], xt[:, i, k * P:(k + 1) * P], ident[:])
                        mm.then_inc(tile_turned, 1)

                    def start(e, pair, par, base):
                        hold(pe, w_split[0], e + 1, passed)

                    def tile(e, par, g):
                        hi, lo = w_hi[par], w_lo[par]
                        pe.wait_ge(xeT_ready, g + 1)
                        for bk in range(4):
                            for i in range(2):
                                c = 2 * bk + i
                                for k in range(KC):
                                    col = slice(k * F + c * P, k * F + (c + 1) * P)
                                    for w, x in ((lo, xeT_hi), (hi, xeT_hi), (hi, xeT_lo)):
                                        mm = pe.matmul(pL[:, bk, i * TM:(i + 1) * TM], w[:, 0, col], x[:, k, :],
                                                       start=(k == 0 and w is lo), stop=(k == KC - 1 and x is xeT_lo))
                            mm.then_inc(l1_done, 1)
                        turn(g + 1)
                        pe.wait_ge(w_split[1], e + 1)
                        pe.wait_ge(y_added, 2 * g + ONE)
                        for i in range(TM // P):
                            rows = slice(i * P, (i + 1) * P)
                            for c in range(FC):
                                if i == 0 and c % 2 == 0:
                                    pe.wait_ge(h_split, 4 * g + c // 2 + 1 + ONE)
                                for s, w in ((h_lo, hi), (h_hi, hi), (h_hi, lo)):
                                    mm = pe.matmul(pY[:, i, 0:D], s[:, c, rows], w[:, 1, c * D:(c + 1) * D],
                                                   start=(c == 0 and s is h_lo), stop=(c == FC - 1 and w is lo))
                            mm.then_inc(l2_done, 1)

                    turn(0)
                    over_tiles(pe, start, tile)

                @block.vector
                def _(dve):
                    dve.sem_inc(h_split, ONE)
                    dve.sem_inc(y_added, ONE)
                    def turn_lo(g):
                        dve.wait_ge(xeT_hi_ready, g + 1)
                        dve.tensor_tensor(xeT_lo[:], pX[:], xeT_hi[:].bitcast(F32), ALU.subtract).then_inc(xeT_ready, 1)
                        dve.wait_ge(tile_in, 16 * (g + 1))
                        dve.tensor_copy(tag[:], xt[:, :, D:XW]).then_inc(tag_saved, 1)

                    def start(e, pair, par, base):
                        if not is_last(e):
                            dve.wait_ge(l2_done, 2 * base + ONE)
                            split_on_dve(dve, e + 1, 1 - par, pair + par + 1)

                    def tile(e, par, g):
                        dve.wait_ge(l2_done, 2 * g + ONE)
                        for bk in range(4):
                            cs = slice(2 * bk, 2 * bk + 2)
                            dve.wait_ge(h_ready, 4 * g + bk + 1)
                            dve.tensor_copy(h_hi[:, cs, :], h[:, cs, :]).then_inc(h_hi_ready, 1)
                            dve.wait_ge(h_hi_ready, 4 * g + bk + 1)
                            dve.tensor_tensor(h_lo[:, cs, :], h[:, cs, :], h_hi[:, cs, :].bitcast(F32),
                                              ALU.subtract).then_inc(h_split, 1)
                        dve.wait_ge(y_left, g + ONE)
                        dve.wait_ge(tag_saved, g + 1)
                        ch = Chain(dve, tag_link, g, TAG_LINKS)
                        me = iota_e[:, bass.ds(e, 1)]
                        ch(dve.tensor_scalar(same[:], tag[:, :, 1], me, None, ALU.is_equal))
                        ch(dve.tensor_scalar(other[:], same[:], -1.0, 1.0, ALU.mult, ALU.add))
                        ch(dve.scalar_tensor_tensor(out=dest[:], in0=other[:], scalar=float(NT), in1=tag[:, :, 0],
                                                    op0=ALU.mult, op1=ALU.add))
                        dve.tensor_tensor(wa[:], same[:], tag[:, :, 2], ALU.mult)
                        ch(dve.tensor_tensor(wb[:], other[:], tag[:, :, 3], ALU.mult))
                        ch(dve.tensor_tensor(weight[:], wa[:], wb[:], ALU.add))
                        turn_lo(g + 1)
                        for i in range(TM // P):
                            dve.wait_ge(l2_done, 2 * g + i + 1 + ONE)
                            dve.tensor_tensor(y[:, i, :], pY[:, i, 0:D],
                                              b2_all[:, bass.ds(e, 1), :].rearrange("p e d -> p (e d)"),
                                              ALU.add).then_inc(y_added, 1)
                            dve.wait_ge(y_added, 2 * g + i + 1 + ONE)
                            dve.tensor_scalar(y[:, i, :], y[:, i, :], weight[:, i:i + 1], None,
                                              ALU.mult).then_inc(y_ready, 1)
                        ch.end()

                    turn_lo(0)
                    over_tiles(dve, start, tile)

        with ExitStack() as octx:
            def so(name, shape, dt):
                return sb(name, shape, dt, octx)

            def sm(name):
                return sem(name, octx)

            SG = 4
            RING = 4
            STEPS = TT // SG
            TURNS = STEPS // RING
            pair = [so(f"pair{i}", [P, 2, SG, D], F32) for i in range(RING)]
            z = [so(f"z{i}", [P, SG, D], F32) for i in range(RING)]
            fstats = so("fstats", [P, 2 * SG, 6], F32)
            fmv = so("fmv", [P, 2 * SG, 2], F32)
            frstd = [so(f"frstd{i}", [P, 2 * SG], F32) for i in range(RING // 2)]
            fshift = [so(f"fshift{i}", [P, 2 * SG], F32) for i in range(RING // 2)]
            fwork = so("fwork", [P, 3, 2 * SG], F32)
            pair_in = [sm(f"pair_in{i}") for i in range(RING)]
            out_link = sm("out_link")
            out_stats = sm("out_stats")
            out_normed = sm("out_normed")
            out_ready = sm("out_ready")
            stored = [sm(f"stored{i}") for i in range(RING)]
            OUT_LINKS = 5 + RSQRT_LINKS
            y_tiles = pair_y.rearrange("(k t p) d -> p k t d", k=2, p=P)
            out_tiles = out_rows.rearrange("(t p) d -> p t d", p=P)

            with nc.Block() as block:

                @block.sync
                def _(sp):
                    for u in range(RING):
                        sp.sem_inc(stored[u], ONE)
                    def load(s, u):
                        for k in range(2):
                            sp.dma_start(pair[u][:, k], y_tiles[:, k, bass.ds(s * SG, SG), :]).then_inc(pair_in[u], 16)

                    def store(s, u):
                        sp.wait_ge(out_ready, s + 1)
                        sp.dma_start(out_tiles[:, bass.ds(s * SG, SG), :], z[u][:]).then_inc(stored[u], 16)

                    for u in range(RING):
                        load(u, u)
                    with sp.Fori(0, TURNS - 1) as r:
                        for u in range(RING):
                            s = RING * r + u
                            sp.wait_ge(out_normed, (s + 1) * SG + ONE)
                            load(s + RING, u)
                            store(s, u)
                    for u in range(RING):
                        store(STEPS - RING + u, u)
                    for u in range(RING):
                        sp.wait_ge(stored[u], 16 * TURNS + ONE)

                @block.vector
                def _(dve):
                    with dve.Fori(0, TURNS) as r:
                        for v in range(RING // 2):
                            ch = Chain(dve, out_link, RING // 2 * r + v, OUT_LINKS, passed)
                            for i in range(2):
                                u = 2 * v + i
                                dve.wait_ge(pair_in[u], 32 * (r + 1))
                                f = pair[u][:, 0]
                                ch(dve.tensor_tensor(f, f, pair[u][:, 1], ALU.add))
                                for t in range(SG):
                                    last = dve.bn_stats(fstats[:, i * SG + t, :], f[:, t, :])
                            ch(last, own=True)
                            for t in range(2 * SG):
                                last = dve.bn_aggr(fmv[:, t, :], fstats[:, t, :])
                            ch(last)
                            dve.wait_ge(out_normed, RING * SG * r + ONE)
                            rsqrt(ch, frstd[v][:], fmv[:, :, 1], [fwork[:, i, :] for i in range(3)])
                            ch(dve.scalar_tensor_tensor(out=fshift[v][:], in0=fmv[:, :, 0], scalar=-1.0,
                                                        in1=frstd[v][:], op0=ALU.mult, op1=ALU.mult))
                            ch.end()
                            dve.tensor_tensor(fshift[v][:], fshift[v][:],
                                              attn_shift[:, bass.ds((RING * r + 2 * v) * SG, 2 * SG)],
                                              ALU.add).then_inc(out_stats, 1)

                @block.scalar
                def _(act):
                    act.sem_inc(out_normed, ONE)
                    with act.Fori(0, TURNS) as r:
                        for u in range(RING):
                            if u % 2 == 0:
                                act.wait_ge(out_stats, RING // 2 * r + u // 2 + 1)
                            act.wait_ge(stored[u], 16 * r + ONE)
                            for t in range(SG):
                                at = u % 2 * SG + t
                                act.activation(z[u][:, t, :], pair[u][:, 0, t, :], ACT.Identity,
                                               bias=fshift[u // 2][:, at:at + 1],
                                               scale=frstd[u // 2][:, at:at + 1]).then_inc(out_normed, 1)

                @block.gpsimd
                def _(pool):
                    with pool.Fori(0, TURNS) as r:
                        for u in range(RING):
                            s = RING * r + u
                            pool.wait_ge(out_normed, (s + 1) * SG + ONE)
                            pool.tensor_tensor(z[u][:], z[u][:], x_all[:, bass.ds(s * SG, SG), :],
                                               ALU.add).then_inc(out_ready, 1)


def low_rows():
    at = np.arange(P) % HID // HK
    return np.where(at == 2, np.float32(-1.0), np.float32(0.0))[:, None]


def constants():
    inv = np.float32(32.0) ** (-np.arange(0, D, 2, dtype=np.float32) / np.float32(D))
    ang = np.arange(L, dtype=np.float32)[None, :] * inv.astype(np.float32)[:, None]
    row, col = np.arange(P)[:, None], np.arange(P)[None, :]
    return {
        "cos_t": np.cos(ang),
        "sin_t": np.sin(ang),
        "ident_c": (row == col).astype(np.float32),
        "mask_c": np.where(col > row, np.float32(MASKED), np.float32(0.0)),
        "tri_c": (row < col).astype(np.float32),
    }


def kernel(**inputs):
    import concourse.bacc as bacc
    from concourse.bass_utils import run_bass_kernel_spmd

    nc = bacc.Bacc("TRN2", target_bir_lowering=False, num_devices=1)
    g = {k: np.asarray(v) for k, v in inputs.items()}
    arrays = {
        "x": g["L0_attn_hidden_states"],
        "wqT": g["L0_attn_Wq"].T,
        "wkT": g["L0_attn_Wk"].T,
        "fc1_w": g["L0_attn_fc1_w"],
        "fc1_b": g["L0_attn_fc1_b"],
        "fc2_wT": g["L0_attn_fc2_w"].T,
        "fc2_b": g["L0_attn_fc2_b"],
        "low_rows": low_rows(),
        "gate_w": g["L0_ffn_gate_w"],
        "gate_b": g["L0_ffn_gate_b"],
        "w1": g["L0_ffn_w1"],
        "b1T": g["L0_ffn_b1"].reshape(NE, FC, P).transpose(2, 0, 1),
        "w2": g["L0_ffn_w2"],
        "b2": g["L0_ffn_b2"],
        **constants(),
    }
    arrays = {k: np.ascontiguousarray(v) for k, v in arrays.items()}
    args = [nc.dram_tensor(k, v.shape, mybir.dt.from_np(v.dtype), kind="ExternalInput").ap() for k, v in arrays.items()]
    args.append(nc.dram_tensor("out", [B, L, D], F32, kind="ExternalOutput").ap())
    build(nc, *args)
    r = run_bass_kernel_spmd(nc, [arrays], core_ids=[0])
    return r.results[0]["out"]
```

```python
from contextlib import ExitStack

import numpy as np
import concourse.bass as bass
from concourse import mybir

F32 = mybir.dt.float32
F32R = mybir.dt.float32r
BF16 = mybir.dt.bfloat16
I32 = mybir.dt.int32
U32 = mybir.dt.uint32
ALU = mybir.AluOpType
ACT = mybir.ActivationFunctionType
AX_X = mybir.AxisListType.X

P = 128
EPS = 1e-5
RSQRT_MAGIC = float(0x5F3759DF)
MASKED = -1e30

B, L, D = 4, 1024, 256
NT = B * L
KC = D // P
TB = L // P
TT = NT // P
INNER = 16
HK = INNER + 1
HID = 64
NE, F = 8, 1024
FC = F // P
TM = 256
TPE = NT // TM
MAXG = 2 * NT // TM + NE
SG = 4
STEPS = TT // SG
PAIRS = STEPS // 2
REGION = NT + TM
XW = D + 4

ONE = 1

C_END, C_TILES, C_ROW = 0, NE, 2 * NE
TAB = MAXG + 2 * TPE + 1
C_ALL = C_ROW + TAB

BATCH_SENT = 2 * TB * 16
SENT_FIRST = TB

RSQRT_LINKS = 10
LN1_LINKS = 1 + RSQRT_LINKS
ROPE_LINKS = 3
HID_LINKS = 3
MID_LINKS = RSQRT_LINKS + 1 + 1 + RSQRT_LINKS
FIRST = 6
ROUTE_LINKS = 11


def hold(eng, sem, value, passed):
    eng.wait_ge(sem, value)
    eng.sem_inc(passed, 1)


class Chain:

    def __init__(self, eng, sem, done, links, passed=None):
        self.eng, self.sem, self.done, self.links, self.n, self.passed = eng, sem, done, links, 0, passed

    def __call__(self, ins, own=False):
        self.n += 1
        ins.then_inc(self.sem, 1)
        self.eng.wait_ge(self.sem, self.done * self.links + self.n)
        if own:
            self.eng.sem_inc(self.passed, 1)

    def end(self):
        assert self.n == self.links, (self.n, self.links)


def rsqrt(ch, out, var, work):
    dve = ch.eng
    v, y, t = work
    ch(dve.tensor_scalar(v, var, EPS, None, ALU.add))
    ch(dve.tensor_scalar(y.bitcast(I32), v.bitcast(I32), -0.5, RSQRT_MAGIC, ALU.mult, ALU.add))
    ch(dve.tensor_tensor(t, y, y, ALU.mult))
    ch(dve.tensor_tensor(t, t, v, ALU.mult))
    ch(dve.tensor_scalar(out, t, 0.375, -1.25, ALU.mult, ALU.add))
    ch(dve.tensor_tensor(t, t, out, ALU.mult))
    ch(dve.scalar_tensor_tensor(out=y, in0=t, scalar=1.875, in1=y, op0=ALU.add, op1=ALU.mult))
    ch(dve.tensor_tensor(t, y, y, ALU.mult))
    ch(dve.scalar_tensor_tensor(out=t, in0=t, scalar=-0.5, in1=v, op0=ALU.mult, op1=ALU.mult))
    ch(dve.scalar_tensor_tensor(out=out, in0=t, scalar=1.5, in1=y, op0=ALU.add, op1=ALU.mult))


def build(nc, x_in, wqT, wkT, fc1_w, fc1_b, fc2_wT, fc2_b, low_rows, gate_w, gate_b, w1, b1T, w2, b2,
          cos_t, sin_t, ident_c, mask_c, tri_c, out):
    x_rows = x_in.rearrange("b l d -> (b l) d")
    out_rows = out.rearrange("b l d -> (b l) d")
    sorted_x = nc.dram_tensor("sorted_x", [NE * REGION, XW], F32).ap()
    sum_y = nc.dram_tensor("sum_y", [NT + TM, D], F32).ap()

    with ExitStack() as ctx:
        def sb(name, shape, dt, c=ctx):
            return c.enter_context(nc.sbuf_tensor(name, shape, dt))

        def sem(name, c=ctx):
            return c.enter_context(nc.semaphore(name))

        x_all = sb("x_all", [P, TT, D], F32)
        attn_shift = sb("attn_shift", [P, TT], F32)
        ident = sb("ident", [P, P], F32)
        b2_all = sb("b2_all", [P, NE, D], F32)
        b1_all = sb("b1_all", [P, NE, FC], F32)
        b1_now = [sb(f"b1_now{i}", [P, FC], F32) for i in range(2)]
        iota_e = sb("iota_e", [P, NE], F32)
        steer = sb("steer", [1, C_ALL], I32)
        w_stage = [sb(f"w_stage{i}", [P, 2, FC * D], F32) for i in range(2)]
        w_hi = [sb("w_hi0", [P, 2, FC * D], F32R), None]
        w_lo = [sb("w_lo0", [P, 2, FC * D], F32R), None]
        weights_in = [sem(f"weights_in{i}") for i in range(2)]
        w_hi_ready = [sem("w1_hi_ready"), sem("w2_hi_ready")]
        w_split = [sem("w1_split"), sem("w2_split")]
        xt = sb("xt", [P, TM // P, XW], F32)
        xrow = sb("xrow", [P, TB, XW], F32)
        slot_i = sb("slot_i", [P, 2 * TB], I32)
        rows_sent = sem("rows_sent")
        tile_in = sem("tile_in")
        b1_taken = sem("b1_taken")
        passed = sem("passed")

        def load_weights(sp, e, par):
            sp.dma_start(w_stage[par][:, 0, :].rearrange("p (k f) -> p k f", k=KC),
                         w1[bass.ds(e, 1), :, :].rearrange("e (k p) f -> p (e k) f", p=P)).then_inc(weights_in[par], 16)
            sp.dma_start(w_stage[par][:, 1, :].rearrange("p (c d) -> p c d", c=FC),
                         w2[bass.ds(e, 1), :, :].rearrange("e (c p) d -> p (e c) d", p=P)).then_inc(weights_in[par], 16)

        def send_rows(pool, which):
            for i in which:
                pool.indirect_dma_start(
                    out=sorted_x, out_offset=bass.IndirectOffsetOnAxis(ap=slot_i[:, i:i + 1], axis=0),
                    in_=xrow[:, i % TB, :], in_offset=None).then_inc(rows_sent, 16)

        def low_part(eng, e, par, i):
            eng.wait_ge(w_hi_ready[i], e + 1)
            eng.tensor_tensor(w_lo[par][:, i, :], w_stage[par][:, i, :],
                              w_hi[par][:, i, :].bitcast(F32), ALU.subtract).then_inc(w_split[i], 1)

        def split_on_act(act, e, par, loads):
            if type(e) is not int or e > 0:
                act.wait_ge(b1_taken, e)
            act.wait_ge(weights_in[par], loads * 32)
            act.activation(w_hi[par][:, 0, :], w_stage[par][:, 0, :], ACT.Copy).then_inc(w_hi_ready[0], 1)
            act.activation(b1_now[par][:], b1_all[:, bass.ds(e, 1), :].rearrange("p e c -> p (e c)"),
                           ACT.Copy).then_inc(b1_taken, 1)

        def split_on_dve(dve, e, par, loads):
            dve.wait_ge(weights_in[par], loads * 32)
            dve.tensor_copy(w_hi[par][:, 1, :], w_stage[par][:, 1, :]).then_inc(w_hi_ready[1], 1)
            low_part(dve, e, par, 0)

        with ExitStack() as actx:
            def sa(name, shape, dt):
                return sb(name, shape, dt, actx)

            def pa(name, shape, dt):
                return actx.enter_context(nc.psum_tensor(name, shape, dt))

            def sm(name):
                return sem(name, actx)

            wqk_hi = sa("wqk_hi", [P, KC, 2, D], F32R)
            wqk_lo = sa("wqk_lo", [P, KC, 2, D], F32R)
            cos_sb = sa("cos_sb", [P, L], BF16)
            sin_sb = sa("sin_sb", [P, L], BF16)
            identb = sa("identb", [P, P], BF16)
            mask = sa("mask", [P, P], BF16)
            tri = sa("tri", [P, P], BF16)
            ones = sa("ones", [P, P], BF16)
            fc1w = sa("fc1w", [P, INNER], F32)
            fc1b = sa("fc1b", [P, INNER], F32)
            fc2 = sa("fc2", [P, D], F32)
            fc2_hi = sa("fc2_hi", [P, D], F32R)
            fc2_parts = sa("fc2_parts", [P, D], F32R)
            lowrow = sa("lowrow", [P, 1], F32)
            gatew = sa("gatew", [P, KC, NE], F32)
            gateb = sa("gateb", [NE, 1], F32)
            ids_i = sa("ids_i", [P, TT], I32)
            ids = sa("ids", [P, TT], F32)
            iota_i = sa("iota_i", [P, NE], I32)
            fill = sa("fill", [P, TM // P, XW], F32)
            fill_i = sa("fill_i", [P, TM // P], I32)

            stats = sa("stats", [P, TB, 6], F32)
            mv = sa("mv", [P, TB, 2], F32)
            rstd = sa("rstd", [P, TB], F32)
            shift = sa("shift", [P, TB], F32)
            nwork = sa("nwork", [P, 3, TB], F32)
            xn = sa("xn", [P, TB, D], F32)
            xT_hi = sa("xT_hi", [P, KC, L], F32R)
            xT_lo = sa("xT_lo", [P, KC, L], F32R)
            qk = sa("qk", [P, 2, KC, L], BF16)
            rope_a = sa("rope_a", [P, 2, L], BF16)
            rope_b = sa("rope_b", [P, 2, L], BF16)
            qkr = sa("qkr", [P, 2, KC, L], BF16)
            probs = sa("probs", [P, L], BF16)
            osum = sa("osum", [P, TB], F32)
            hid16 = sa("hid16", [P, TB, INNER], F32)
            hid = sa("hid", [P, TB, HID], F32)
            hidT = sa("hidT", [P, TB // 2, P], F32R)
            mstats = sa("mstats", [P, TB, 6], F32)
            mmv = sa("mmv", [P, TB, 2], F32)
            mrstd = sa("mrstd", [P, 2, TB], F32)
            mshift = sa("mshift", [P, TB], F32)
            mwork = sa("mwork", [P, 3, TB], F32)
            x3T = sa("x3T", [P, KC, L], F32)
            wqk = x3T[:].rearrange("p k n -> p (k n)")[:, 0:KC * 2 * D].rearrange("p (k i d) -> p k i d", k=KC, i=2)
            logitsT = sa("logitsT", [NE, 2, 512], F32)
            top8 = sa("top8", [P, TB, 8], F32)
            idx8 = sa("idx8", [P, TB, 8], U32)
            idxf = sa("idxf", [P, 2, TB], F32)
            onehot = sa("onehot", [P, 2, TB, NE], F32)
            chosen = sa("chosen", [P, TB, NE], BF16)
            scan_in = sa("scan_in", [P, NE, TB + 1], F32)
            scan_keep = sa("scan_keep", [P, NE, TB + 1], F32)
            carry = sa("carry", [P, NE, TB + 1], F32)
            pos = sa("pos", [P, TB, NE], F32)
            slot_w = sa("slot_w", [P, 2, TB, NE], F32)
            slot = sa("slot", [P, 2 * TB], F32)
            gdiff = sa("gdiff", [P, TB], F32)
            gexp = sa("gexp", [P, TB], F32)
            gden = sa("gden", [P, TB], F32)
            cnt = sa("cnt", [P, 6, NE + 1], F32)
            cnt_i = sa("cnt_i", [P, 2, NE], I32)
            gm = sa("gm", [P, 5, NE], F32)
            gcol = sa("gcol", [P, 4], F32)
            gword = sa("gword", [P, 1], F32)

            pT = pa("pT", [P, 2, 512], F32)
            pP = pa("pP", [P, 2, 512], F32)
            pS = pa("pS", [P, 4, 512], F32)
            pA = pS[:, :, :].rearrange("p b (u d) -> p (b u) d", d=D)
            pLogT = pP[0:NE]
            pLog = pT[:, 0, 0:TB * NE]
            pWord = pP[0:1, 0, 0:P]
            pRank = pP[:, 1, 0:TB * NE]
            pTot = pP[:, 1, TB * NE:2 * TB * NE]

            x_first = [sm("x_first0"), sm("x_first1")]
            x_second = sm("x_second")
            x_rest = sm("x_rest")
            ident_in = sm("ident_in")
            wqk_in = sm("wqk_in")
            consts_in = sm("consts_in")
            b2_in = sm("b2_in")
            tables_in = sm("tables_in")
            pool_set = sm("pool_set")
            set_up = sm("set_up")
            x_measured = sm("x_measured")
            ln1_link = sm("ln1_link")
            xn_stats = sm("xn_stats")
            xn_ready = sm("xn_ready")
            xn_turned = sm("xn_turned")
            xT_hi_ready = sm("xT_hi_ready")
            xT_ready = sm("xT_ready")
            projected = sm("projected")
            qk_ready = sm("qk_ready")
            rope_link = sm("rope_link")
            roped = sm("roped")
            scored = sm("scored")
            summed = sm("summed")
            mid_link = sm("mid_link")
            hid_link = sm("hid_link")
            attn_measured = sm("attn_measured")
            attn_aggregated = sm("attn_aggregated")
            hid_ready = sm("hid_ready")
            hid_turned = sm("hid_turned")
            hidT_ready = sm("hidT_ready")
            mlp_done = sm("mlp_done")
            attn_added = sm("attn_added")
            x3_stats = sm("x3_stats")
            x3_ready = sm("x3_ready")
            x3_turned = sm("x3_turned")
            x3T_ready = sm("x3T_ready")
            logitsT_done = sm("logitsT_done")
            logitsT_ready = sm("logitsT_ready")
            logits_done = sm("logits_done")
            route_link = sm("route_link")
            gdiff_ready = sm("gdiff_ready")
            gexp_ready = sm("gexp_ready")
            chosen_ready = sm("chosen_ready")
            ranked = sm("ranked")
            ranks_read = sm("ranks_read")
            rows_ready = sm("rows_ready")
            rows_left = sm("rows_left")
            steer_link = sm("steer_link")
            steer_ready = sm("steer_ready")
            ends_ready = sm("ends_ready")
            words_ready = sm("words_ready")
            words_turned = sm("words_turned")
            ends_filled = sm("ends_filled")
            odd_ends_filled = sm("odd_ends_filled")
            sums_cleared = sm("sums_cleared")

            CONSTS = 6 + 12
            with nc.Block() as block:

                def fill_ends(eng, experts, filled):
                    eng.wait_ge(ends_ready, 1)
                    for e in experts:
                        end = eng.value_load(steer[0:1, C_END + e:C_END + e + 1], min_val=e * REGION,
                                             max_val=e * REGION + NT)
                        eng.dma_start(sorted_x[bass.ds(end, TM), :].rearrange("(a p) c -> p a c", p=P),
                                      fill[:]).then_inc(filled, 16)
                    eng.wait_ge(filled, 16 * len(experts))

                @block.sync
                def _(sp):
                    for h in range(2):
                        sp.dma_start(x_all[:, h * TB // 2:(h + 1) * TB // 2, :],
                                     x_rows[h * L // 2:(h + 1) * L // 2, :].rearrange("(t p) d -> p t d", p=P)
                                     ).then_inc(x_first[h], 16)
                    sp.dma_start(ident[:], ident_c).then_inc(ident_in, 16)
                    for i, w in enumerate((wqT, wkT)):
                        sp.dma_start(wqk[:, :, i, :], w.rearrange("(k p) d -> p k d", p=P)).then_inc(wqk_in, 16)
                    sp.dma_start(x_all[:, TB:2 * TB, :], x_rows[L:2 * L, :].rearrange("(t p) d -> p t d", p=P)
                                 ).then_inc(x_second, 16)
                    load_weights(sp, 0, 0)
                    for dst, src in ((fc1w[:], fc1_w.rearrange("i o -> o i").to_broadcast([P, INNER])),
                                     (fc1b[:], fc1_b.rearrange("(o i) -> o i", o=1).to_broadcast([P, INNER])),
                                     (gatew[:], gate_w.rearrange("(k p) e -> p k e", p=P)),
                                     (gateb[:], gate_b.rearrange("(e o) -> e o", o=1)),
                                     (lowrow[:], low_rows),
                                     (b1_all[:], b1T)):
                        sp.dma_start(dst, src).then_inc(consts_in, 16)
                    for j in range(2):
                        for i in range(3):
                            at = HID * j + HK * i
                            sp.dma_start(fc2[at:at + INNER, :], fc2_wT).then_inc(consts_in, 16)
                            sp.dma_start(fc2[at + INNER:at + HK, :],
                                         fc2_b.rearrange("(o d) -> o d", o=1)).then_inc(consts_in, 16)
                    for b in range(2, B):
                        sp.dma_start(x_all[:, b * TB:(b + 1) * TB, :],
                                     x_rows[b * L:(b + 1) * L, :].rearrange("(t p) d -> p t d", p=P)).then_inc(x_rest, 16)
                    sp.dma_start(b2_all[:].rearrange("p e d -> p (e d)"),
                                 b2.rearrange("e d -> (e d)").rearrange("(o n) -> o n", o=1).to_broadcast([P, NE * D])
                                 ).then_inc(b2_in, 16)
                    load_weights(sp, 1, 1)
                    sp.wait_ge(pool_set, 8)
                    sp.dma_start(sum_y.rearrange("(t p) d -> p t d", p=P),
                                 fill[:, 0:1, 0:D].to_broadcast([P, TT + TM // P, D])
                                 ).then_inc(sums_cleared, 16)
                    fill_ends(sp, range(0, NE, 2), ends_filled)
                    sp.wait_ge(sums_cleared, 16)
                    sp.wait_ge(b2_in, 16)

                @block.gpsimd
                def _(pool):
                    pool.sem_inc(rows_left, ONE)
                    for dst, src in ((cos_sb, cos_t), (sin_sb, sin_t), (mask, mask_c), (tri, tri_c)):
                        pool.dma_start(dst[:], src).then_inc(tables_in, 16)
                    pool.memset(ones[:], 1.0).then_inc(pool_set, 1)
                    pool.memset(hid[:], 0.0).then_inc(pool_set, 1)
                    pool.memset(fill[:], 0.0).then_inc(pool_set, 1)
                    pool.iota(ids_i[:], pattern=[[P, TT]], base=0, channel_multiplier=1).then_inc(pool_set, 1)
                    pool.iota(iota_i[:], pattern=[[1, NE]], base=0, channel_multiplier=0).then_inc(pool_set, 1)
                    pool.iota(fill_i[:], pattern=[[P, TM // P]], base=NT, channel_multiplier=1).then_inc(pool_set, 1)
                    pool.wait_ge(pool_set, 6)
                    pool.tensor_copy(fill[:, :, D], fill_i[:]).then_inc(pool_set, 1)
                    pool.memset(fill[:, :, D + 1:D + 2], -1.0).then_inc(pool_set, 1)
                    low_part(pool, 0, 0, 1)

                    with pool.Fori(0, B - 1) as b:
                        hold(pool, rows_ready, b + 1, passed)
                        send_rows(pool, range(2 * TB))
                        hold(pool, rows_sent, (b + 1) * BATCH_SENT, rows_left)
                    pool.wait_ge(rows_ready, B)
                    send_rows(pool, range(SENT_FIRST))

                @block.scalar
                def _(act):
                    act.sem_inc(gexp_ready, ONE)
                    def norm_x(b):
                        act.wait_ge(xn_stats, b + 1)
                        act.wait_ge(xn_turned, b * 4)
                        for t in range(TB):
                            act.activation(xn[:, t, :], x_all[:, b * TB + t, :], ACT.Identity, bias=shift[:, t:t + 1],
                                           scale=rstd[:, t:t + 1]).then_inc(xn_ready, 1)

                    def turn_hi(b):
                        act.wait_ge(projected, b * 8)
                        for n in range(2 * KC):
                            h, k = n // KC, n % KC
                            act.wait_ge(xn_turned, b * 4 + n + 1)
                            act.activation(xT_hi[:, k, h * 512:(h + 1) * 512], pT[:, n % 2, :],
                                           ACT.Copy).then_inc(xT_hi_ready, 1)

                    def take_qk(b, roped_before):
                        act.wait_ge(roped, 2 * roped_before)
                        for n in range(8):
                            h, i, m = n // 4, (n // 2) % 2, n % 2
                            act.wait_ge(projected, b * 8 + n + 1)
                            act.activation(qk[:, i, m, h * 512:(h + 1) * 512], pP[:, n % 2, :],
                                           ACT.Copy).then_inc(qk_ready, 1)

                    def sum_exps(b, tiles):
                        act.wait_ge(hid_ready, b + ONE)
                        for t in tiles:
                            act.wait_ge(scored, b * TB + t + 1)
                            act.wait_ge(summed, b * TB + t)
                            n = (t + 1) * P
                            act.activation(probs[:, 0:n],
                                           pS[:, 2 * (t % 2):2 * (t % 2) + 2, :].rearrange("p b n -> p (b n)")[:, 0:n],
                                           ACT.Exp, scale=1.0 / D ** 0.5,
                                           accum_out=osum[:, t:t + 1]).then_inc(summed, 1)

                    def take_hid(c):
                        act.wait_ge(hid_turned, c + 1 + ONE)
                        act.activation(hidT[:].rearrange("p g n -> p (g n)"), pT[:, 0, :],
                                       ACT.Copy).then_inc(hidT_ready, 1)

                    def norm_x3(c):
                        act.wait_ge(x3_stats, c + 1)
                        act.wait_ge(rows_left, c + ONE)
                        for h in range(2):
                            for t in range(4 * h, 4 * h + 4):
                                act.activation(xrow[:, t, 0:D], x_all[:, c * TB + t, :], ACT.Identity,
                                               bias=mshift[:, t:t + 1],
                                               scale=mrstd[:, 1, t:t + 1]).then_inc(x3_ready, 1)
                            for k in range(KC):
                                act.wait_ge(x3_turned, c * 4 + KC * h + k + 1)
                                act.activation(x3T[:, k, h * 512:(h + 1) * 512], pT[:, k, :],
                                               ACT.Copy).then_inc(x3T_ready, 1)
                        act.wait_ge(logits_done, c)
                        for h in range(2):
                            act.wait_ge(logitsT_done, c * 2 + h + 1)
                            act.activation(logitsT[:, h, :], pLogT[:, h, :], ACT.Identity,
                                           bias=gateb[:, 0:1]).then_inc(logitsT_ready, 1)

                    def weigh(c):
                        act.wait_ge(gdiff_ready, c + 1)
                        act.activation(gexp[:], gdiff[:], ACT.Exp).then_inc(gexp_ready, 1)

                    norm_x(0)
                    turn_hi(0)
                    take_qk(0, 0)
                    act.wait_ge(consts_in, 16 * CONSTS)
                    split_on_act(act, 0, 0, 1)
                    sum_exps(0, range(TB))
                    with act.Fori(0, B - 1) as j:
                        take_hid(j)
                        norm_x(j + 1)
                        turn_hi(j + 1)
                        take_qk(j + 1, j + 1)
                        norm_x3(j)
                        sum_exps(j + 1, range(FIRST))
                        weigh(j)
                        sum_exps(j + 1, range(FIRST, TB))
                    take_hid(B - 1)
                    norm_x3(B - 1)
                    weigh(B - 1)
                    fill_ends(act, range(1, NE, 2), odd_ends_filled)

                @block.tensor
                def _(pe):
                    pe.sem_inc(hid_turned, ONE)
                    def turn_x(b):
                        for n in range(2 * KC):
                            h, k = n // KC, n % KC
                            if n >= 2:
                                pe.wait_ge(xT_ready, b * 4 + n - 1)
                            for u in range(4):
                                t = 4 * h + u
                                if k == 0:
                                    pe.wait_ge(xn_ready, b * TB + t + 1)
                                mm = pe.transpose(pT[:, n % 2, u * P:(u + 1) * P], xn[:, t, k * P:(k + 1) * P], ident[:])
                            mm.then_inc(xn_turned, 1)

                    def project(b, routed):
                        pe.wait_ge(ranks_read, routed + ONE)
                        for n in range(8):
                            h, i, m = n // 4, (n // 2) % 2, n % 2
                            pe.wait_ge(xT_ready, b * 4 + 2 * (h + 1))
                            if n >= 2:
                                pe.wait_ge(qk_ready, b * 8 + n - 1)
                            tok = slice(h * 512, (h + 1) * 512)
                            mo = slice(m * P, (m + 1) * P)
                            for k in range(KC):
                                for w, x in ((wqk_lo, xT_hi), (wqk_hi, xT_hi), (wqk_hi, xT_lo)):
                                    mm = pe.matmul(pP[:, n % 2, :], w[:, k, i, mo], x[:, k, tok],
                                                   start=(k == 0 and w is wqk_lo), stop=(k == KC - 1 and x is xT_lo))
                            mm.then_inc(projected, 1)

                    def score(b, tiles):
                        pe.wait_ge(attn_added, b * TB)
                        for t in tiles:
                            if t == tiles[0]:
                                pe.wait_ge(roped, 2 * b + (1 if tiles[-1] < TB // 2 else 2))
                            if t >= 2:
                                pe.wait_ge(summed, b * TB + t - 1)
                            keys = (t + 1) * P
                            for a in range(0, keys, 512):
                                n = min(512, keys - a)
                                bank = pS[:, 2 * (t % 2) + a // 512, :]
                                last = a + n == keys
                                for m in range(KC):
                                    mm = pe.matmul(bank[:, 0:n], qkr[:, 0, m, t * P:(t + 1) * P],
                                                   qkr[:, 1, m, a:a + n], start=(m == 0), stop=(m == KC - 1 and not last))
                                if last:
                                    mm = pe.matmul(bank[:, n - P:n], identb[:], mask[:], start=False, stop=True)
                            mm.then_inc(scored, 1)

                    def attention_mlp(c):
                        pe.wait_ge(hid_ready, c + 1 + ONE)
                        for g in range(TB // 2):
                            mm = pe.transpose(pT[:, 0, g * P:(g + 1) * P],
                                              hid[:, 2 * g:2 * g + 2, :].rearrange("p t h -> p (t h)"), ident[:])
                        mm.then_inc(hid_turned, 1)
                        pe.wait_ge(hidT_ready, c + 1)
                        pe.wait_ge(summed, (c + 1) * TB)
                        for g in range(TB // 2):
                            for j in range(2):
                                rows = slice(HID * j, HID * j + 3 * HK)
                                mm = pe.matmul(pA[:, 4 * j + g, :], hidT[rows, g, :], fc2_parts[rows, :],
                                               start=True, stop=True)
                            if g % 2 == 1:
                                mm.then_inc(mlp_done, 1)

                    def gate(c, fronts):
                        for h in range(2):
                            for k in range(KC):
                                if h == 1:
                                    pe.wait_ge(x3T_ready, c * 4 + k + 1)
                                for u in range(4):
                                    t = 4 * h + u
                                    if k == 0:
                                        pe.wait_ge(x3_ready, c * TB + t + 1)
                                    mm = pe.transpose(pT[:, k, u * P:(u + 1) * P], xrow[:, t, k * P:(k + 1) * P], ident[:])
                                mm.then_inc(x3_turned, 1)
                            if h == 0:
                                pe.wait_ge(qk_ready, fronts * 8)
                            for k in range(KC):
                                pe.wait_ge(x3T_ready, c * 4 + KC * h + k + 1)
                                mm = pe.matmul(pLogT[:, h, :], gatew[:, k, :], x3T[:, k, h * 512:(h + 1) * 512],
                                               start=(k == 0), stop=(k == KC - 1))
                            mm.then_inc(logitsT_done, 1)
                        for t in range(TB):
                            if t % 4 == 0:
                                hold(pe, logitsT_ready, c * 2 + t // 4 + 1, passed)
                            mm = pe.transpose(pLog[:, t * NE:(t + 1) * NE], logitsT[:, t // 4, t % 4 * P:(t % 4 + 1) * P],
                                              ident[0:NE, 0:NE])
                        mm.then_inc(logits_done, 1)

                    def rank(c):
                        pe.wait_ge(chosen_ready, c + 1)
                        ch = chosen[:].rearrange("p t e -> p (t e)")
                        pe.matmul(pRank, tri[:], ch, start=True, stop=True)
                        pe.matmul(pTot, ones[:], ch, start=True, stop=True).then_inc(ranked, 1)

                    pe.wait_ge(ident_in, 16)
                    turn_x(0)
                    pe.wait_ge(set_up, 2)
                    project(0, 0)
                    pe.wait_ge(tables_in, 64)
                    pe.wait_ge(pool_set, 8)
                    pe.wait_ge(set_up, 8)
                    score(0, range(TB // 2))
                    score(0, range(TB // 2, TB))
                    with pe.Fori(0, B - 1) as j:
                        attention_mlp(j)
                        turn_x(j + 1)
                        project(j + 1, j)
                        gate(j, j + 2)
                        score(j + 1, range(FIRST))
                        rank(j)
                        score(j + 1, range(FIRST, TB))
                    attention_mlp(B - 1)
                    gate(B - 1, B)
                    rank(B - 1)
                    pe.wait_ge(words_ready, 1)
                    pe.matmul(pWord, gword[:], ident[:], start=True, stop=True).then_inc(words_turned, 1)

                @block.vector
                def _(dve):
                    dve.sem_inc(hid_ready, ONE)
                    dve.sem_inc(ranks_read, ONE)
                    def measure_x(b, tiles=range(TB)):
                        for t in tiles:
                            s = dve.bn_stats(stats[:, t, :], x_all[:, b * TB + t, :])
                        if tiles[-1] == TB - 1:
                            s.then_inc(x_measured, 1)

                    def scale_x(b):
                        hold(dve, x_measured, b + 1, passed)
                        ch = Chain(dve, ln1_link, b, LN1_LINKS, passed)
                        for t in range(TB):
                            s = dve.bn_aggr(mv[:, t, :], stats[:, t, :])
                        ch(s)
                        dve.wait_ge(xn_ready, b * TB)
                        rsqrt(ch, rstd[:], mv[:, :, 1], [nwork[:, i, :] for i in range(3)])
                        dve.scalar_tensor_tensor(out=shift[:], in0=mv[:, :, 0], scalar=-1.0, in1=rstd[:],
                                                 op0=ALU.mult, op1=ALU.mult).then_inc(xn_stats, 1)
                        ch.end()

                    def turn_lo(b, pieces=range(2 * KC)):
                        for n in pieces:
                            h, k = n // KC, n % KC
                            dve.wait_ge(xT_hi_ready, b * 4 + n + 1)
                            tok = slice(h * 512, (h + 1) * 512)
                            dve.tensor_tensor(xT_lo[:, k, tok], pT[:, n % 2, :], xT_hi[:, k, tok].bitcast(F32),
                                              ALU.subtract).then_inc(xT_ready, 1)

                    def rope(call, b, taken, n0, n1):
                        dve.wait_ge(qk_ready, taken)
                        dve.wait_ge(scored, b * TB)
                        n = n1 - n0
                        co = cos_sb[:, n0:n1].rearrange("p (o n) -> p o n", o=1).to_broadcast([P, 2, n])
                        si = sin_sb[:, n0:n1].rearrange("p (o n) -> p o n", o=1).to_broadcast([P, 2, n])
                        ch = Chain(dve, rope_link, call, ROPE_LINKS)
                        for m, op in ((0, ALU.subtract), (1, ALU.add)):
                            dve.tensor_tensor(rope_a[:, :, 0:n], qk[:, :, m, n0:n1], co, ALU.mult)
                            ch(dve.tensor_tensor(rope_b[:, :, 0:n], qk[:, :, 1 - m, n0:n1], si, ALU.mult))
                            last = dve.tensor_tensor(qkr[:, :, m, n0:n1], rope_a[:, :, 0:n], rope_b[:, :, 0:n], op)
                            if m == 0:
                                ch(last)
                        ch.end()
                        last.then_inc(roped, 2 * n // L)

                    def hidden(c):
                        dve.wait_ge(summed, (c + 1) * TB)
                        dve.wait_ge(hid_turned, c + ONE)
                        ch = Chain(dve, hid_link, c, HID_LINKS)
                        ch(dve.tensor_tensor(hid16[:], osum[:].rearrange("p (t o) -> p t o", o=1).to_broadcast([P, TB, INNER]),
                                             fc1w[:].rearrange("p (o i) -> p o i", o=1).to_broadcast([P, TB, INNER]),
                                             ALU.mult))
                        ch(dve.tensor_tensor(hid16[:], hid16[:],
                                             fc1b[:].rearrange("p (o i) -> p o i", o=1).to_broadcast([P, TB, INNER]),
                                             ALU.add))
                        hi, lo, hi2 = (hid[:, :, HK * i:HK * i + INNER].bitcast(F32R) for i in range(3))
                        dve.tensor_scalar(hi2, hid16[:], 0.0, None, ALU.max)
                        ch(dve.tensor_scalar(hi, hid16[:], 0.0, None, ALU.max))
                        dve.scalar_tensor_tensor(out=lo, in0=hid16[:], scalar=0.0, in1=hi.bitcast(F32),
                                                 op0=ALU.max, op1=ALU.subtract).then_inc(hid_ready, 1)
                        ch.end()

                    def stats_attn(c):
                        for g in range(TB // 2):
                            if g % 2 == 0:
                                dve.wait_ge(mlp_done, c * (TB // 4) + g // 2 + 1)
                            for j in range(2):
                                s = dve.bn_stats(mstats[:, 2 * g + j, :], pA[:, 4 * j + g, :])
                        s.then_inc(attn_measured, 1)

                    def aggregate():
                        for t in range(TB):
                            s = dve.bn_aggr(mmv[:, t, :], mstats[:, t, :])
                        return s

                    def aggregate_attn(c):
                        hold(dve, attn_measured, c + 1, passed)
                        aggregate().then_inc(attn_aggregated, 1)

                    def mid(c):
                        work = [mwork[:, i, :] for i in range(3)]
                        ch = Chain(dve, mid_link, c, MID_LINKS, passed)
                        dve.wait_ge(attn_aggregated, c + 1)
                        rsqrt(ch, mrstd[:, 0, :], mmv[:, :, 1], work)
                        dve.scalar_tensor_tensor(out=attn_shift[:, bass.ds(c * TB, TB)], in0=mmv[:, :, 0], scalar=-1.0,
                                                 in1=mrstd[:, 0, :], op0=ALU.mult, op1=ALU.mult)
                        for t in range(TB):
                            xt = x_all[:, c * TB + t, :]
                            s = dve.scalar_tensor_tensor(out=xt, in0=pA[:, 4 * (t % 2) + t // 2, :],
                                                         scalar=mrstd[:, 0, t:t + 1], in1=xt,
                                                         op0=ALU.mult, op1=ALU.add).then_inc(attn_added, 1)
                        hold(dve, attn_added, (c + 1) * TB, passed)
                        for t in range(TB):
                            s = dve.bn_stats(mstats[:, t, :], x_all[:, c * TB + t, :])
                        ch(s, own=True)
                        ch(aggregate())
                        rsqrt(ch, mrstd[:, 1, :], mmv[:, :, 1], work)
                        dve.wait_ge(x3_ready, c * TB)
                        dve.scalar_tensor_tensor(out=mshift[:], in0=mmv[:, :, 0], scalar=-1.0, in1=mrstd[:, 1, :],
                                                 op0=ALU.mult, op1=ALU.mult).then_inc(x3_stats, 1)
                        ch.end()

                    def route(c):
                        ch = Chain(dve, route_link, c, ROUTE_LINKS, passed)
                        hold(dve, logits_done, c + 1, passed)
                        for t in range(TB):
                            s = dve.max(top8[:, t, :], pLog[:, t * NE:(t + 1) * NE])
                        ch(s, own=True)
                        for t in range(TB):
                            s = dve.max_index(idx8[:, t, :], top8[:, t, :], pLog[:, t * NE:(t + 1) * NE])
                        ch(s)
                        dve.wait_ge(gexp_ready, c + ONE)
                        dve.tensor_tensor(gdiff[:], top8[:, :, 1], top8[:, :, 0], ALU.subtract).then_inc(gdiff_ready, 1)
                        ch(dve.tensor_copy(idxf[:], idx8[:, :, 0:2].rearrange("p t k -> p k t")))
                        io = iota_e[:].rearrange("p (o e) -> p o e", o=1).to_broadcast([P, TB, NE])
                        for k in range(2):
                            s = dve.tensor_tensor(onehot[:, k], io,
                                                  idxf[:, k, :].rearrange("p (t o) -> p t o", o=1).to_broadcast([P, TB, NE]),
                                                  ALU.is_equal)
                        ch(s)
                        dve.tensor_tensor(chosen[:], onehot[:, 0], onehot[:, 1], ALU.add).then_inc(chosen_ready, 1)
                        dve.wait_ge(rows_left, c + ONE)
                        dve.wait_ge(x3_ready, (c + 1) * TB)
                        dve.tensor_copy(xrow[:, :, D], ids[:, bass.ds(c * TB, TB)])
                        dve.tensor_copy(xrow[:, :, D + 1], idxf[:, 0, :])
                        dve.wait_ge(ranked, c + 1)
                        ch(dve.tensor_copy(scan_in[:, :, 1:TB + 1], pTot.rearrange("p (t e) -> p e t", e=NE)))
                        ch(dve.tensor_tensor_scan(carry[:].rearrange("p e t -> p (e t)"),
                                                  scan_keep[:].rearrange("p e t -> p (e t)"),
                                                  scan_in[:].rearrange("p e t -> p (e t)"), 0.0, ALU.mult, ALU.add))
                        dve.tensor_tensor(pos[:], pRank.rearrange("p (t e) -> p t e", e=NE),
                                          carry[:, :, 0:TB].rearrange("p e t -> p t e"), ALU.add).then_inc(ranks_read, 1)
                        dve.tensor_copy(scan_in[:, :, 0:1], carry[:, :, TB:TB + 1])
                        dve.wait_ge(ranks_read, c + 1 + ONE)
                        for k in range(2):
                            s = dve.tensor_tensor(slot_w[:, k], onehot[:, k], pos[:], ALU.mult)
                        ch(s)
                        ch(dve.tensor_reduce(slot[:], slot_w[:].rearrange("p k t e -> p (k t) e"), AX_X, ALU.add))
                        ch(dve.tensor_copy(slot_i[:], slot[:]))
                        dve.wait_ge(gexp_ready, c + 1 + ONE)
                        ch(dve.tensor_scalar(gden[:], gexp[:], 1.0, None, ALU.add))
                        ch(dve.reciprocal(xrow[:, :, D + 2], gden[:]))
                        dve.tensor_tensor(xrow[:, :, D + 3], gexp[:], xrow[:, :, D + 2],
                                          ALU.mult).then_inc(rows_ready, 1)
                        ch.end()

                    def steer_table():
                        n = [0]

                        def ch(ins):
                            n[0] += 1
                            ins.then_inc(steer_link, 1)
                            dve.wait_ge(steer_link, n[0])

                        end, count, tiles, incl, base, keep = (cnt[:, i, 0:NE] for i in range(6))
                        ch(dve.tensor_copy(end, carry[:, :, TB]))
                        dve.tensor_copy(steer[:, C_END:C_END + NE], end[0:1, :]).then_inc(ends_ready, 1)
                        done = gm[:, 4, :]
                        dve.tensor_scalar(done, carry[:, :, 0], -float(TM), None, ALU.add)
                        dve.memset(keep, 1.0)
                        ch(dve.scalar_tensor_tensor(out=count, in0=iota_e[:], scalar=-float(REGION), in1=end,
                                                    op0=ALU.mult, op1=ALU.add))
                        ch(dve.tensor_scalar(cnt_i[:, 0, :], count, float(TM - 1), None, ALU.add))
                        ch(dve.tensor_scalar(cnt_i[:, 1, :], cnt_i[:, 0, :], int(np.log2(TM)), None,
                                             ALU.arith_shift_right))
                        ch(dve.tensor_copy(tiles, cnt_i[:, 1, :]))
                        ch(dve.tensor_tensor_scan(incl, keep, tiles, 0.0, ALU.mult, ALU.add))
                        ch(dve.tensor_tensor(base, incl, tiles, ALU.subtract))
                        dve.scalar_tensor_tensor(out=steer[:, C_TILES:C_TILES + NE], in0=base[0:1, :], scalar=32.0,
                                                 in1=tiles[0:1, :], op0=ALU.mult, op1=ALU.add)
                        g = ids[:, 0:1]
                        mine, row, late, tmp = (gm[:, i, :] for i in range(4))
                        dve.tensor_scalar(mine, base, g, None, ALU.is_le)
                        ch(dve.tensor_scalar(tmp, base, g, None, ALU.subtract))
                        dve.scalar_tensor_tensor(out=mine, in0=incl, scalar=g, in1=mine, op0=ALU.is_gt, op1=ALU.mult)
                        ch(dve.tensor_scalar(tmp, tmp, -float(TM), None, ALU.mult))
                        ch(dve.scalar_tensor_tensor(out=row, in0=iota_e[:], scalar=float(REGION), in1=tmp,
                                                    op0=ALU.mult, op1=ALU.add))
                        ch(dve.tensor_tensor(late, row, done, ALU.is_gt))
                        ch(dve.scalar_tensor_tensor(out=row, in0=row, scalar=2.0, in1=late, op0=ALU.mult, op1=ALU.add))
                        ch(dve.tensor_tensor(row, row, mine, ALU.mult))
                        ch(dve.tensor_reduce(gcol[:, 0:2], gm[:, 0:2, :], AX_X, ALU.add))
                        dve.tensor_scalar(gcol[:, 2:3], gcol[:, 0:1], -1.0, 1.0, ALU.mult, ALU.add)
                        ch(dve.tensor_scalar(gcol[:, 3:4], end[:, 0:1], 2.0, 1.0, ALU.mult, ALU.add))
                        dve.scalar_tensor_tensor(out=gword[:], in0=gcol[:, 2:3], scalar=gcol[:, 3:4],
                                                 in1=gcol[:, 1:2], op0=ALU.mult, op1=ALU.add).then_inc(words_ready, 1)
                        dve.wait_ge(words_turned, 1)
                        dve.tensor_copy(steer[:, C_ROW:C_ROW + TAB], pWord[:, 0:TAB]).then_inc(steer_ready, 1)

                    for h in range(2):
                        dve.wait_ge(x_first[h], 16)
                        measure_x(0, range(h * TB // 2, (h + 1) * TB // 2))
                    scale_x(0)
                    dve.wait_ge(wqk_in, 32)
                    dve.tensor_copy(wqk_hi[:], wqk).then_inc(set_up, 1)
                    dve.wait_ge(set_up, 1)
                    dve.tensor_tensor(wqk_lo[:], wqk, wqk_hi[:].bitcast(F32), ALU.subtract).then_inc(set_up, 1)
                    turn_lo(0)
                    dve.wait_ge(pool_set, 8)
                    for i in range(0, 3, 2):
                        at = HK * i + INNER
                        dve.tensor_scalar(hid[:, :, at], hid[:, :, HID - 1], 1.0, None, ALU.add)
                    dve.tensor_copy(ids[:], ids_i[:])
                    dve.memset(scan_keep[:], 1.0)
                    dve.tensor_copy(iota_e[:], iota_i[:]).then_inc(set_up, 1)
                    dve.wait_ge(set_up, 3)
                    dve.tensor_scalar(scan_in[:, :, 0], iota_e[:], float(REGION), None, ALU.mult)
                    dve.memset(scan_keep[:, :, 0:1], 0.0)
                    dve.wait_ge(ident_in, 16)
                    dve.tensor_copy(identb[:], ident[:]).then_inc(set_up, 1)
                    dve.wait_ge(x_second, 16)
                    measure_x(1)
                    scale_x(1)
                    dve.wait_ge(tables_in, 64)
                    rope(0, 0, 4, 0, L // 2)
                    dve.wait_ge(consts_in, 16 * CONSTS)
                    for j in range(2):
                        rows = slice(HID * j, HID * j + 3 * HK)
                        dve.tensor_copy(fc2_hi[rows, :], fc2[rows, :]).then_inc(set_up, 1)
                    dve.wait_ge(set_up, 6)
                    for j in range(2):
                        rows = slice(HID * j, HID * j + 3 * HK)
                        dve.scalar_tensor_tensor(out=fc2_parts[rows, :], in0=fc2_hi[rows, :].bitcast(F32),
                                                 scalar=lowrow[rows, 0:1], in1=fc2[rows, :],
                                                 op0=ALU.mult, op1=ALU.add).then_inc(set_up, 1)
                    rope(1, 0, 8, L // 2, L)
                    split_on_dve(dve, 0, 0, 1)
                    dve.wait_ge(x_rest, 16 * (B - 2))

                    def batch(j, more):
                        hidden(j)
                        if more:
                            measure_x(j + 2)
                        stats_attn(j)
                        turn_lo(j + 1, range(0, 2))
                        aggregate_attn(j)
                        turn_lo(j + 1, range(2, 4))
                        mid(j)
                        rope(j + 2, j + 1, (j + 2) * 8, 0, L)
                        if more:
                            scale_x(j + 2)
                        route(j)

                    with dve.Fori(0, B - 2) as j:
                        batch(j, True)
                    batch(B - 2, False)
                    hidden(B - 1)
                    stats_attn(B - 1)
                    aggregate_attn(B - 1)
                    mid(B - 1)
                    route(B - 1)
                    steer_table()

        y_sum = [sb(f"y_sum{s}", [P, SG, D], F32) for s in range(2)]
        sum_in = [sem(f"sum_in{s}") for s in range(STEPS)]
        y_tiles = sum_y.rearrange("(t p) d -> p t d", p=P)

        def load_sums(sp, s):
            sp.dma_start(y_sum[s][:], y_tiles[:, s * SG:(s + 1) * SG, :]).then_inc(sum_in[s], 16)

        with ExitStack() as ectx:
            def se(name, shape, dt):
                return sb(name, shape, dt, ectx)

            def pe_sum(name, shape, dt):
                return ectx.enter_context(nc.psum_tensor(name, shape, dt))

            def sm(name):
                return sem(name, ectx)

            w_hi[1] = se("w_hi1", [P, 2, FC * D], F32R)
            w_lo[1] = se("w_lo1", [P, 2, FC * D], F32R)
            xeT_hi = se("xeT_hi", [P, KC, TM], F32R)
            xeT_lo = se("xeT_lo", [P, KC, TM], F32R)
            h = se("h", [P, FC, TM], F32)
            h_hi = se("h_hi", [P, FC, TM], F32R)
            h_lo = se("h_lo", [P, FC, TM], F32R)
            tag = se("tag", [P, TM // P, 4], F32)
            other = se("other", [P, TM // P], F32)
            same = se("same", [P, TM // P], F32)
            wa = se("wa", [P, TM // P], F32)
            wb = se("wb", [P, TM // P], F32)
            weight = se("weight", [P, TM // P], F32)
            dest = se("dest", [P, TM // P], I32)
            y = se("y", [P, TM // P, D], F32)
            pL = pe_sum("pL", [P, 4, 512], F32)
            pX = pe_sum("pX", [P, KC, TM], F32)
            pY = pe_sum("pY", [P, 2, 512], F32)

            tile_turned = sm("tile_turned")
            tag_saved = sm("tag_saved")
            xeT_hi_ready = sm("xeT_hi_ready")
            xeT_ready = sm("xeT_ready")
            l1_done = sm("l1_done")
            h_ready = sm("h_ready")
            h_hi_ready = sm("h_hi_ready")
            h_split = sm("h_split")
            l2_done = sm("l2_done")
            tag_link = sm("tag_link")
            y_added = sm("y_added")
            y_ready = sm("y_ready")
            y_sent = sm("y_sent")
            y_left = sm("y_left")
            TAG_LINKS = 4

            def is_last(e):
                return type(e) is int and e == NE - 1

            def over_tiles(eng, start, tile):
                def expert(pair, par):
                    e = pair * 2 + par
                    both = eng.value_load(steer[0:1, bass.ds(C_TILES + e, 1)], min_val=0, max_val=MAXG * 32 + TPE)
                    n, base = both & 31, both >> 5
                    if start:
                        start(e, pair, par, base)

                    def bits(k):
                        with eng.If(n >= 1 << k):
                            with eng.If((n & (1 << k)) > 0):
                                first = base if k == 0 else base + (n & ((1 << k) - 1))
                                if k < 3:
                                    for v in range(1 << k):
                                        tile(e, par, first + v)
                                else:
                                    with eng.Fori(0, 1 << k - 2) as v:
                                        for i in range(4):
                                            tile(e, par, first + 4 * v + i)
                            if 2 << k <= TPE:
                                bits(k + 1)

                    bits(0)

                with eng.Fori(0, NE // 2 - 1) as pair:
                    for par in range(2):
                        expert(pair, par)
                for par in range(2):
                    expert(NE // 2 - 1, par)

            with nc.Block() as block:

                @block.sync
                def _(sp):
                    def tile_word(sp, g):
                        return sp.value_load(steer[0:1, bass.ds(C_ROW + g, 1)], min_val=0,
                                             max_val=2 * (NE * REGION - TM) - 1)

                    def load_tile(sp, word):
                        hold(sp, rows_sent, (word & 1) * BATCH_SENT + (B - 1) * BATCH_SENT, passed)
                        sp.dma_start(xt[:], sorted_x[bass.ds(word >> 1, TM), :].rearrange("(a p) c -> p a c", p=P)
                                     ).then_inc(tile_in, 16)

                    def start(e, pair, par, base):
                        if type(e) is not int:
                            for i in range(2):
                                sp.wait_ge(w_split[i], e + 1)
                            load_weights(sp, e + 2, par)

                    def tile(e, par, g):
                        word = tile_word(sp, g + 1)
                        hold(sp, tile_turned, g + 1, passed)
                        hold(sp, tag_saved, g + 1, passed)
                        load_tile(sp, word)

                    both = sp.value_load(steer[0:1, C_TILES + NE - 1:C_TILES + NE], min_val=0, max_val=MAXG * 32 + TPE)
                    load_tile(sp, tile_word(sp, 0))
                    over_tiles(sp, start, tile)
                    sp.wait_ge(y_left, (both >> 5) + (both & 31) + ONE)
                    for s in range(2):
                        load_sums(sp, s)

                @block.gpsimd
                def _(pool):
                    pool.sem_inc(y_left, ONE)
                    send_rows(pool, range(SENT_FIRST, 2 * TB))
                    def start(e, pair, par, base):
                        if not is_last(e):
                            pool.wait_ge(l2_done, 2 * base + ONE)
                            low_part(pool, e + 1, 1 - par, 1)

                    def tile(e, par, g):
                        for i in range(TM // P):
                            hold(pool, y_ready, 2 * g + i + 1, passed)
                            pool.indirect_dma_start(
                                out=sum_y, out_offset=bass.IndirectOffsetOnAxis(ap=dest[:, i:i + 1], axis=0),
                                in_=y[:, i, :], in_offset=None,
                                compute_op=ALU.add).then_inc(y_sent, 16)
                        hold(pool, y_sent, (g + 1) * 32, y_left)

                    over_tiles(pool, start, tile)

                @block.scalar
                def _(act):
                    def turn_hi(g):
                        act.wait_ge(tile_turned, g + 1)
                        act.activation(xeT_hi[:], pX[:], ACT.Copy).then_inc(xeT_hi_ready, 1)

                    def start(e, pair, par, base):
                        if not is_last(e):
                            act.wait_ge(l2_done, 2 * base + ONE)
                            split_on_act(act, e + 1, 1 - par, pair + par + 1)

                    def tile(e, par, g):
                        act.wait_ge(b1_taken, e + 1)
                        act.wait_ge(h_split, 4 * g + ONE)
                        for bk in range(4):
                            act.wait_ge(l1_done, 4 * g + bk + 1)
                            for i in range(2):
                                c = 2 * bk + i
                                a = act.activation(h[:, c, :], pL[:, bk, i * TM:(i + 1) * TM], ACT.Gelu,
                                                   bias=b1_now[par][:, c:c + 1])
                            a.then_inc(h_ready, 1)
                        turn_hi(g + 1)

                    turn_hi(0)
                    over_tiles(act, start, tile)

                @block.tensor
                def _(pe):
                    pe.sem_inc(l2_done, ONE)
                    def turn(g):
                        pe.wait_ge(tile_in, 16 * (g + 1))
                        for k in range(KC):
                            for i in range(TM // P):
                                mm = pe.transpose(pX[:, k, i * P:(i + 1) * P], xt[:, i, k * P:(k + 1) * P], ident[:])
                        mm.then_inc(tile_turned, 1)

                    def start(e, pair, par, base):
                        hold(pe, w_split[0], e + 1, passed)

                    def tile(e, par, g):
                        hi, lo = w_hi[par], w_lo[par]
                        pe.wait_ge(xeT_ready, g + 1)
                        for bk in range(4):
                            for i in range(2):
                                c = 2 * bk + i
                                for k in range(KC):
                                    col = slice(k * F + c * P, k * F + (c + 1) * P)
                                    for w, x in ((lo, xeT_hi), (hi, xeT_hi), (hi, xeT_lo)):
                                        mm = pe.matmul(pL[:, bk, i * TM:(i + 1) * TM], w[:, 0, col], x[:, k, :],
                                                       start=(k == 0 and w is lo), stop=(k == KC - 1 and x is xeT_lo))
                            mm.then_inc(l1_done, 1)
                        turn(g + 1)
                        pe.wait_ge(w_split[1], e + 1)
                        pe.wait_ge(y_added, 2 * g + ONE)
                        for i in range(TM // P):
                            rows = slice(i * P, (i + 1) * P)
                            for c in range(FC):
                                if i == 0 and c % 2 == 0:
                                    pe.wait_ge(h_split, 4 * g + c // 2 + 1 + ONE)
                                for s, w in ((h_lo, hi), (h_hi, hi), (h_hi, lo)):
                                    mm = pe.matmul(pY[:, i, 0:D], s[:, c, rows], w[:, 1, c * D:(c + 1) * D],
                                                   start=(c == 0 and s is h_lo), stop=(c == FC - 1 and w is lo))
                            mm.then_inc(l2_done, 1)

                    turn(0)
                    over_tiles(pe, start, tile)

                @block.vector
                def _(dve):
                    dve.sem_inc(h_split, ONE)
                    dve.sem_inc(y_added, ONE)
                    def turn_lo(g):
                        dve.wait_ge(xeT_hi_ready, g + 1)
                        dve.tensor_tensor(xeT_lo[:], pX[:], xeT_hi[:].bitcast(F32), ALU.subtract).then_inc(xeT_ready, 1)
                        dve.wait_ge(tile_in, 16 * (g + 1))
                        dve.tensor_copy(tag[:], xt[:, :, D:XW]).then_inc(tag_saved, 1)

                    def start(e, pair, par, base):
                        if not is_last(e):
                            dve.wait_ge(l2_done, 2 * base + ONE)
                            split_on_dve(dve, e + 1, 1 - par, pair + par + 1)

                    def tile(e, par, g):
                        dve.wait_ge(l2_done, 2 * g + ONE)
                        for bk in range(4):
                            cs = slice(2 * bk, 2 * bk + 2)
                            dve.wait_ge(h_ready, 4 * g + bk + 1)
                            dve.tensor_copy(h_hi[:, cs, :], h[:, cs, :]).then_inc(h_hi_ready, 1)
                            dve.wait_ge(h_hi_ready, 4 * g + bk + 1)
                            dve.tensor_tensor(h_lo[:, cs, :], h[:, cs, :], h_hi[:, cs, :].bitcast(F32),
                                              ALU.subtract).then_inc(h_split, 1)
                        dve.wait_ge(y_left, g + ONE)
                        dve.wait_ge(tag_saved, g + 1)
                        ch = Chain(dve, tag_link, g, TAG_LINKS)
                        me = iota_e[:, bass.ds(e, 1)]
                        ch(dve.tensor_scalar(same[:], tag[:, :, 1], me, None, ALU.is_equal))
                        ch(dve.tensor_scalar(other[:], same[:], -1.0, 1.0, ALU.mult, ALU.add))
                        dve.tensor_copy(dest[:], tag[:, :, 0])
                        dve.tensor_tensor(wa[:], same[:], tag[:, :, 2], ALU.mult)
                        ch(dve.tensor_tensor(wb[:], other[:], tag[:, :, 3], ALU.mult))
                        ch(dve.tensor_tensor(weight[:], wa[:], wb[:], ALU.add))
                        turn_lo(g + 1)
                        for i in range(TM // P):
                            dve.wait_ge(l2_done, 2 * g + i + 1 + ONE)
                            dve.tensor_tensor(y[:, i, :], pY[:, i, 0:D],
                                              b2_all[:, bass.ds(e, 1), :].rearrange("p e d -> p (e d)"),
                                              ALU.add).then_inc(y_added, 1)
                            dve.wait_ge(y_added, 2 * g + i + 1 + ONE)
                            dve.tensor_scalar(y[:, i, :], y[:, i, :], weight[:, i:i + 1], None,
                                              ALU.mult).then_inc(y_ready, 1)
                        ch.end()

                    turn_lo(0)
                    over_tiles(dve, start, tile)

        with ExitStack() as octx:
            def so(name, shape, dt):
                return sb(name, shape, dt, octx)

            def sm(name):
                return sem(name, octx)

            y_sum += [so(f"y_sum{s}", [P, SG, D], F32) for s in range(2, STEPS)]
            z = [so(f"z{s}", [P, SG, D], F32) for s in range(STEPS)]
            fstats = so("fstats", [P, 2 * SG, 6], F32)
            fmv = so("fmv", [P, 2 * SG, 2], F32)
            frstd = so("frstd", [P, TT], F32)
            fshift = so("fshift", [P, TT], F32)
            fwork = so("fwork", [P, 3, 2 * SG], F32)
            out_link = sm("out_link")
            out_stats = sm("out_stats")
            out_normed = sm("out_normed")
            out_ready = sm("out_ready")
            last_normed = sm("last_normed")
            last_ready = sm("last_ready")
            stored = sm("stored")
            OUT_LINKS = 3 + RSQRT_LINKS
            out_tiles = out_rows.rearrange("(t p) d -> p t d", p=P)

            def residual(eng, s, normed, count, done):
                eng.wait_ge(normed, count)
                eng.tensor_tensor(z[s][:], z[s][:], x_all[:, s * SG:(s + 1) * SG, :], ALU.add).then_inc(done, 1)

            with nc.Block() as block:

                @block.sync
                def _(sp):
                    for s in range(2, STEPS):
                        load_sums(sp, s)
                    for s in range(STEPS):
                        if s < STEPS - 1:
                            sp.wait_ge(out_ready, s + 1)
                        else:
                            sp.wait_ge(last_ready, 1)
                        sp.dma_start(out_tiles[:, s * SG:(s + 1) * SG, :], z[s][:]).then_inc(stored, 16)
                    sp.wait_ge(stored, 16 * STEPS)

                @block.vector
                def _(dve):
                    for v in range(PAIRS):
                        ch = Chain(dve, out_link, v, OUT_LINKS)
                        two = slice(2 * v * SG, 2 * (v + 1) * SG)
                        for i in range(2):
                            dve.wait_ge(sum_in[2 * v + i], 16)
                            for t in range(SG):
                                last = dve.bn_stats(fstats[:, i * SG + t, :], y_sum[2 * v + i][:, t, :])
                        ch(last)
                        for t in range(2 * SG):
                            last = dve.bn_aggr(fmv[:, t, :], fstats[:, t, :])
                        ch(last)
                        rsqrt(ch, frstd[:, two], fmv[:, :, 1], [fwork[:, i, :] for i in range(3)])
                        ch(dve.scalar_tensor_tensor(out=fshift[:, two], in0=fmv[:, :, 0], scalar=-1.0,
                                                    in1=frstd[:, two], op0=ALU.mult, op1=ALU.mult))
                        ch.end()
                        dve.tensor_tensor(fshift[:, two], fshift[:, two], attn_shift[:, two], ALU.add).then_inc(out_stats, 1)
                    s = STEPS - 1
                    dve.wait_ge(out_stats, PAIRS)
                    for t in range(SG):
                        at = s * SG + t
                        last = dve.tensor_scalar(z[s][:, t, :], y_sum[s][:, t, :], frstd[:, at:at + 1],
                                                 fshift[:, at:at + 1], ALU.mult, ALU.add)
                    last.then_inc(last_normed, 1)
                    residual(dve, s, last_normed, 1, last_ready)

                @block.scalar
                def _(act):
                    for s in range(STEPS - 1):
                        if s % 2 == 0:
                            act.wait_ge(out_stats, s // 2 + 1)
                        for t in range(SG):
                            at = s * SG + t
                            last = act.activation(z[s][:, t, :], y_sum[s][:, t, :], ACT.Identity,
                                                  bias=fshift[:, at:at + 1], scale=frstd[:, at:at + 1])
                        last.then_inc(out_normed, 1)

                @block.gpsimd
                def _(pool):
                    for s in range(STEPS - 1):
                        residual(pool, s, out_normed, s + 1, out_ready)


def low_rows():
    at = np.arange(P) % HID // HK
    return np.where(at == 2, np.float32(-1.0), np.float32(0.0))[:, None]


def constants():
    inv = np.float32(32.0) ** (-np.arange(0, D, 2, dtype=np.float32) / np.float32(D))
    ang = np.arange(L, dtype=np.float32)[None, :] * inv.astype(np.float32)[:, None]
    row, col = np.arange(P)[:, None], np.arange(P)[None, :]
    return {
        "cos_t": np.cos(ang),
        "sin_t": np.sin(ang),
        "ident_c": (row == col).astype(np.float32),
        "mask_c": np.where(col > row, np.float32(MASKED), np.float32(0.0)),
        "tri_c": (row < col).astype(np.float32),
    }


def kernel(**inputs):
    import concourse.bacc as bacc
    from concourse.bass_utils import run_bass_kernel_spmd

    nc = bacc.Bacc("TRN2", target_bir_lowering=False, num_devices=1)
    g = {k: np.asarray(v) for k, v in inputs.items()}
    arrays = {
        "x": g["L0_attn_hidden_states"],
        "wqT": g["L0_attn_Wq"].T,
        "wkT": g["L0_attn_Wk"].T,
        "fc1_w": g["L0_attn_fc1_w"],
        "fc1_b": g["L0_attn_fc1_b"],
        "fc2_wT": g["L0_attn_fc2_w"].T,
        "fc2_b": g["L0_attn_fc2_b"],
        "low_rows": low_rows(),
        "gate_w": g["L0_ffn_gate_w"],
        "gate_b": g["L0_ffn_gate_b"],
        "w1": g["L0_ffn_w1"],
        "b1T": g["L0_ffn_b1"].reshape(NE, FC, P).transpose(2, 0, 1),
        "w2": g["L0_ffn_w2"],
        "b2": g["L0_ffn_b2"],
        **constants(),
    }
    arrays = {k: np.ascontiguousarray(v) for k, v in arrays.items()}
    args = [nc.dram_tensor(k, v.shape, mybir.dt.from_np(v.dtype), kind="ExternalInput").ap() for k, v in arrays.items()]
    args.append(nc.dram_tensor("out", [B, L, D], F32, kind="ExternalOutput").ap())
    build(nc, *args)
    r = run_bass_kernel_spmd(nc, [arrays], core_ids=[0])
    return r.results[0]["out"]
```
